# Optimizing a Trainium2 kernel written in Bass

```python
import numpy as np
import jax
import jax.numpy as jnp

def _softmax(x, axis=-1):
    return jax.nn.softmax(x, axis=axis)

def _gelu(x):
    return jax.nn.gelu(x, approximate=True)

def _silu(x):
    return jax.nn.silu(x)

def _sigmoid(x):
    return jax.nn.sigmoid(x)

def _layernorm(x, axis=-1, eps=1e-05):
    m = jnp.mean(x, axis=axis, keepdims=True)
    v = jnp.var(x, axis=axis, keepdims=True)
    return (x - m) / jnp.sqrt(v + eps)

def _scatter_add(tgt, idx, src, axis=0):
    return tgt.at[idx].add(src)

def _segment_sum(src, seg, n):
    return jax.ops.segment_sum(src, seg, n)
kernel_name = 'mk_seq_preln_d1_jaxref_r8_be46c2'

def setup_inputs(seed: int=0):
    np.random.seed(seed)
    _w = jnp.asarray

    def _L0_attn_setup():
        import jax, jax.numpy as jnp
        import numpy as np
        B, L, D = (8, 256, 128)
        LN_EPS = 1e-05
        WKV_EPS = 1e-08

        def _ln(x, g, b):
            m = x.mean(-1, keepdims=True)
            v = x.var(-1, keepdims=True)
            return (x - m) * jax.lax.rsqrt(v + LN_EPS) * g + b

        def _shift(x):
            return jnp.pad(x, ((0, 0), (1, 0), (0, 0)))[:, :-1]

        def _wkv(k, v, time_decay, time_first):
            ew = jnp.exp(-jnp.exp(time_decay))
            e0 = jnp.exp(time_first + k[:, 0])
            a0 = e0 * v[:, 0]
            b0 = e0

            def step(carry, kv):
                a, b = carry
                kt, vt = kv
                ek = jnp.exp(kt)
                a = ew * a + ek * vt
                b = ew * b + ek
                return ((a, b), a / (b + WKV_EPS))
            xs = (jnp.swapaxes(k[:, 1:], 0, 1), jnp.swapaxes(v[:, 1:], 0, 1))
            _, outs = jax.lax.scan(step, (a0, b0), xs)
            out0 = (a0 / (b0 + WKV_EPS))[:, None]
            return jnp.concatenate([out0, jnp.swapaxes(outs, 0, 1)], axis=1)
        key = jax.random.key(seed)
        ks = jax.random.split(key, 10)
        s = 1.0 / np.sqrt(D)

        def w(k, shape, scale):
            return jax.random.normal(k, shape, jnp.float32) * scale
        return {'x': jax.random.normal(ks[0], (B, L, D), jnp.float32), 'ln1_g': jnp.ones((D,), jnp.float32), 'ln1_b': jnp.zeros((D,), jnp.float32), 'Wk': w(ks[1], (D, D), s), 'Wv': w(ks[2], (D, D), s), 'Wr': w(ks[3], (D, D), s), 'Wo': w(ks[4], (D, D), s), 'time_decay': w(ks[5], (D,), 0.1), 'time_first': w(ks[6], (D,), 0.1), 'mix_k': jnp.full((D,), 0.5, jnp.float32), 'mix_v': jnp.full((D,), 0.5, jnp.float32), 'mix_r': jnp.full((D,), 0.5, jnp.float32), 'ln2_g': jnp.ones((D,), jnp.float32), 'ln2_b': jnp.zeros((D,), jnp.float32), 'Wfk': w(ks[7], (D, 4 * D), s), 'Wfv': w(ks[8], (4 * D, D), 1.0 / np.sqrt(4 * D)), 'Wfr': w(ks[9], (D, D), s)}
    _L0_attn_in = _L0_attn_setup()

    def _L0_ffn_setup():
        import jax, jax.numpy as jnp
        import numpy as np
        TOP_K = 2
        key = jax.random.key(seed)
        k1, k2, k3, k4 = jax.random.split(key, 4)
        B, T, D, H, E = (2, 256, 128, 256, 8)
        x = jax.random.normal(k1, (B, T, D), dtype=jnp.float32)
        w12 = jax.random.normal(k2, (E, 2 * H, D), dtype=jnp.float32) * D ** (-0.5)
        w3 = jax.random.normal(k3, (E, D, H), dtype=jnp.float32) * H ** (-0.5)
        gate_w = jax.random.normal(k4, (E, D), dtype=jnp.float32) * D ** (-0.5)
        return {'x': x, 'w12': w12, 'w3': w3, 'gate_w': gate_w}
    _L0_ffn_in = _L0_ffn_setup()
    _d = {'L0_attn_x': _L0_attn_in['x'], 'L0_attn_ln1_g': _L0_attn_in['ln1_g'], 'L0_attn_ln1_b': _L0_attn_in['ln1_b'], 'L0_attn_Wk': _L0_attn_in['Wk'], 'L0_attn_Wv': _L0_attn_in['Wv'], 'L0_attn_Wr': _L0_attn_in['Wr'], 'L0_attn_Wo': _L0_attn_in['Wo'], 'L0_attn_time_decay': _L0_attn_in['time_decay'], 'L0_attn_time_first': _L0_attn_in['time_first'], 'L0_attn_mix_k': _L0_attn_in['mix_k'], 'L0_attn_mix_v': _L0_attn_in['mix_v'], 'L0_attn_mix_r': _L0_attn_in['mix_r'], 'L0_attn_ln2_g': _L0_attn_in['ln2_g'], 'L0_attn_ln2_b': _L0_attn_in['ln2_b'], 'L0_attn_Wfk': _L0_attn_in['Wfk'], 'L0_attn_Wfv': _L0_attn_in['Wfv'], 'L0_attn_Wfr': _L0_attn_in['Wfr'], 'L0_ffn_w12': _L0_ffn_in['w12'], 'L0_ffn_w3': _L0_ffn_in['w3'], 'L0_ffn_gate_w': _L0_ffn_in['gate_w']}
    _x0 = _d['L0_attn_x']
    _d['L0_attn_x'] = jax.random.normal(jax.random.fold_in(jax.random.key(seed), 1), (16, 256, 128), dtype=_x0.dtype)
    del _x0
    return _d

def reference(L0_attn_x, L0_attn_ln1_g, L0_attn_ln1_b, L0_attn_Wk, L0_attn_Wv, L0_attn_Wr, L0_attn_Wo, L0_attn_time_decay, L0_attn_time_first, L0_attn_mix_k, L0_attn_mix_v, L0_attn_mix_r, L0_attn_ln2_g, L0_attn_ln2_b, L0_attn_Wfk, L0_attn_Wfv, L0_attn_Wfr, L0_ffn_w12, L0_ffn_w3, L0_ffn_gate_w):

    def _L0_attn_ref(x, ln1_g, ln1_b, Wk, Wv, Wr, Wo, time_decay, time_first, mix_k, mix_v, mix_r, ln2_g, ln2_b, Wfk, Wfv, Wfr):
        import jax, jax.numpy as jnp
        import numpy as np
        B, L, D = (8, 256, 128)
        LN_EPS = 1e-05
        WKV_EPS = 1e-08

        def _ln(x, g, b):
            m = x.mean(-1, keepdims=True)
            v = x.var(-1, keepdims=True)
            return (x - m) * jax.lax.rsqrt(v + LN_EPS) * g + b

        def _shift(x):
            return jnp.pad(x, ((0, 0), (1, 0), (0, 0)))[:, :-1]

        def _wkv(k, v, time_decay, time_first):
            ew = jnp.exp(-jnp.exp(time_decay))
            e0 = jnp.exp(time_first + k[:, 0])
            a0 = e0 * v[:, 0]
            b0 = e0

            def step(carry, kv):
                a, b = carry
                kt, vt = kv
                ek = jnp.exp(kt)
                a = ew * a + ek * vt
                b = ew * b + ek
                return ((a, b), a / (b + WKV_EPS))
            xs = (jnp.swapaxes(k[:, 1:], 0, 1), jnp.swapaxes(v[:, 1:], 0, 1))
            _, outs = jax.lax.scan(step, (a0, b0), xs)
            out0 = (a0 / (b0 + WKV_EPS))[:, None]
            return jnp.concatenate([out0, jnp.swapaxes(outs, 0, 1)], axis=1)
        xn = _ln(x, ln1_g, ln1_b)
        xp = _shift(xn)
        k = (xn * mix_k + xp * (1.0 - mix_k)) @ Wk
        v = (xn * mix_v + xp * (1.0 - mix_v)) @ Wv
        r = jax.nn.sigmoid((xn * mix_r + xp * (1.0 - mix_r)) @ Wr)
        wkv = _wkv(k, v, time_decay, time_first)
        x = x + r * wkv @ Wo
        yn = _ln(x, ln2_g, ln2_b)
        yp = _shift(yn)
        kk = jnp.square(jax.nn.relu((0.5 * yn + 0.5 * yp) @ Wfk))
        rr = jax.nn.sigmoid(yn @ Wfr)
        return x + rr * (kk @ Wfv)

    def _L0_ffn_ref(x, w12, w3, gate_w):
        import jax, jax.numpy as jnp
        import numpy as np
        TOP_K = 2
        E = gate_w.shape[0]
        H = w3.shape[-1]
        scores = jnp.einsum('btd,ed->bte', x, gate_w)
        topk_scores, topk_idx = jax.lax.top_k(scores, TOP_K)
        topk_probs = jax.nn.softmax(topk_scores, axis=-1)
        total_probs = jnp.sum(jax.nn.one_hot(topk_idx, E, dtype=topk_probs.dtype) * topk_probs[..., None], axis=-2)
        h12 = jnp.einsum('btd,ehd->bteh', x, w12)
        h1, h2 = (h12[..., :H], h12[..., H:])
        hidden = jax.nn.silu(h1) * h2
        expert_out = jnp.einsum('bteh,edh->bted', hidden, w3)
        y = jnp.sum(total_probs[..., None] * expert_out, axis=-2)
        return y
    x = L0_attn_x
    x = x + _L0_attn_ref(_layernorm(x, axis=-1), L0_attn_ln1_g, L0_attn_ln1_b, L0_attn_Wk, L0_attn_Wv, L0_attn_Wr, L0_attn_Wo, L0_attn_time_decay, L0_attn_time_first, L0_attn_mix_k, L0_attn_mix_v, L0_attn_mix_r, L0_attn_ln2_g, L0_attn_ln2_b, L0_attn_Wfk, L0_attn_Wfv, L0_attn_Wfr)
    x = x + _L0_ffn_ref(_layernorm(x, axis=-1), L0_ffn_w12, L0_ffn_w3, L0_ffn_gate_w)
    return x

_drawn_inputs = setup_inputs


def setup_inputs(seed=0):
    import zlib

    import numpy as np

    out = dict(_drawn_inputs(seed))
    spreads = {'L0_attn_ln1_g': (1.0, 0.2),
     'L0_attn_ln1_b': (0.0, 0.1),
     'L0_attn_mix_k': (0.5, 0.6),
     'L0_attn_mix_v': (0.5, 0.2),
     'L0_attn_mix_r': (0.5, 0.6),
     'L0_attn_ln2_g': (1.0, 0.2),
     'L0_attn_ln2_b': (0.0, 0.1)}
    factors = {'L0_attn_time_decay': 2.895, 'L0_attn_time_first': 200.0}
    for name, (base, spread) in spreads.items():
        noise = np.random.default_rng([zlib.crc32(name.encode()), seed]).standard_normal(out[name].shape)
        drawn = base * np.exp(spread * noise) if base else spread * noise
        out[name] = jnp.asarray(drawn.astype(out[name].dtype))
    for name, factor in factors.items():
        out[name] = (out[name] * factor).astype(out[name].dtype)
    return out
```

```python
import concourse.bass as bass
from concourse import mybir
from concourse.alu_op_type import AluOpType as ALU
from contextlib import ExitStack

F32 = mybir.dt.float32
I32 = mybir.dt.int32
U32 = mybir.dt.uint32
ACT = mybir.ActivationFunctionType

B, L, D = 16, 256, 128
P = 128
TOKENS = B * L
TILES = TOKENS // P
TPC = 4
CT = TPC * P
BPC = CT // L
CHUNKS = TILES // TPC
FFN = 4 * D
FB = FFN // P
E, H = 8, 256
LN_EPS = 1e-5
WKV_EPS = 1e-8
VEC = {n: i for i, n in enumerate(
    ["ln1_g", "ln1_b", "mix_k", "mix_v", "mix_r", "ln2_g", "ln2_b", "time_decay", "time_first"])}
WOFF = {}
_at = 0
for _n, _w in [("Wk", D), ("Wv", D), ("Wr", D), ("Wo", D), ("Wfr", D), ("Wfk", FFN), ("Wfv", FFN), ("gate", E)]:
    WOFF[_n] = (_at, _at + _w)
    _at += _w
WCOLS = _at
TOPK = 2
ROW = D + 2
REGION = TOKENS + P
SLOTS = TOKENS * TOPK // P + E
IDLE = E
RESULTS = TOKENS * TOPK
NOWHERE = 2 * RESULTS


def build(nc, x_in, w_in, v_in, w12_in, w3_in, out):
    ctx = ExitStack()
    with ctx:
        def sb(name, shape, dt=F32):
            return ctx.enter_context(nc.sbuf_tensor(name, shape, dt))

        def bank(name):
            return ctx.enter_context(nc.psum_tensor(name, [P, CT], F32))

        def sem(name):
            return ctx.enter_context(nc.semaphore(name))

        x_all = sb("x_all", [P, TILES, D])
        w_sb = sb("w_sb", [P, WCOLS])
        vec = sb("vec", [P, len(VEC)])
        ident = sb("ident", [P, P])
        decay = sb("decay", [P, CT])
        ew = sb("ew", [P, 2])
        neg_half = sb("neg_half", [P, 2 * TPC])

        st1 = sb("st1", [P, TPC, 6]); mv1 = sb("mv1", [P, TPC, 2]); dm1 = sb("dm1", [P, TPC])
        st2 = sb("st2", [P, TPC, 6]); mv2 = sb("mv2", [P, TPC, 2]); dm2 = sb("dm2", [P, TPC])
        st3 = sb("st3", [P, TPC, 6]); mv3 = sb("mv3", [P, TPC, 2]); dm3 = sb("dm3", [P, TPC])
        var1 = sb("var1", [P, 2 * TPC]); rs1 = sb("rs1", [P, 2 * TPC])
        var2 = sb("var2", [P, TPC]); rs2 = sb("rs2", [P, TPC])
        var3 = sb("var3", [P, TPC]); rs3 = sb("rs3", [P, TPC])
        nm1 = sb("nm1", [P, TPC])
        z1 = sb("z1", [P, TPC, D]); y1 = sb("y1", [P, TPC, D])
        xn = sb("xn", [P, BPC, L + 1]); dif = sb("dif", [P, BPC, L])
        mixed = [sb(f"mixed_{n}", [P, BPC, L]) for n in "kvr"]
        ek = sb("ek", [P, BPC, L]); ekv = sb("ekv", [P, CT])
        tr = sb("tr", [P, CT]); num = sb("num", [P, CT]); den = sb("den", [P, CT])
        rden = sb("rden", [P, CT]); gated = sb("gated", [P, CT]); rw = sb("rw", [P, CT])
        x2 = sb("x2", [P, TPC, D]); z2 = sb("z2", [P, TPC, D])
        yn = sb("yn", [P, BPC, L + 1]); ysum = sb("ysum", [P, BPC, L])
        trr = sb("trr", [P, CT]); hr = sb("hr", [P, FB, CT]); kk = sb("kk", [P, FB, CT])
        ffn = sb("ffn", [P, CT]); x3 = sb("x3", [P, TPC, D]); xm = sb("xm", [P, TPC, D]); xmT = sb("xmT", [P, CT])

        rows = sb("rows", [P, TPC, TOPK, ROW])
        pad = sb("pad", [P, ROW])
        tri = sb("tri", [P, P]); ones = sb("ones", [P, P])
        rev = sb("rev", [P, TPC, E]); region = sb("region", [P, TPC, E]); ids = sb("ids", [P, TILES, TOPK], I32)
        sc = sb("sc", [P, TPC, E]); eq = sb("eq", [P, TPC, E]); low = sb("low", [P, TPC])
        best = sb("best", [P, TOPK, TPC]); hot = sb("hot", [P, TOPK, TPC, E]); both = sb("both", [P, TPC, E])
        gap = sb("gap", [P, TPC]); egap = sb("egap", [P, TPC]); esum = sb("esum", [P, TPC]); prob = sb("prob", [P, TPC, TOPK])
        seen = sb("seen", [P, E]); chunk_seen = sb("chunk_seen", [P, E])
        spot = sb("spot", [P, TPC, E]); spots = sb("spots", [P, TOPK, TPC, E]); pos = sb("pos", [P, TOPK, TPC], U32)
        total = sb("total", [P, E]); total_i = sb("total_i", [P, E], I32)
        ntile_i = sb("ntile_i", [P, E], I32); ntile = sb("ntile", [P, E]); cum = sb("cum", [P, E])
        ones_e = sb("ones_e", [P, E]); slot_no = sb("slot_no", [P, SLOTS])
        past = sb("past", [P, SLOTS, E]); past_tiles = sb("past_tiles", [P, SLOTS, E])
        slot_e = sb("slot_e", [P, SLOTS]); slot_first = sb("slot_first", [P, SLOTS])
        slot_row = sb("slot_row", [P, SLOTS], I32); slot_w = sb("slot_w", [P, SLOTS], I32)
        w12_sb = sb("w12_sb", [P, E * 2 * H]); w3_sb = sb("w3_sb", [P, E * 2 * D])
        xg = [sb(f"xg{n}", [P, ROW]) for n in range(4)]
        xgT = [sb(f"xgT{n}", [P, P]) for n in range(2)]
        th = [sb(f"th{n}", [P, H]) for n in range(2)]
        gate_h = sb("gate_h", [P, H]); hid = [sb(f"hid{n}", [P, H]) for n in range(2)]
        hidT = [sb(f"hidT{n}", [P, 2, P]) for n in range(2)]
        yo = [sb(f"yo{n}", [P, D]) for n in range(4)]
        o_all = sb("o_all", [P, TILES, TOPK, D])

        rows_d = nc.dram_tensor("rows_d", [E * REGION + IDLE * P, ROW], F32, kind="Internal").ap()
        res_d = nc.dram_tensor("res_d", [RESULTS, D], F32, kind="Internal").ap()

        p_tr = bank("p_tr"); p_k = bank("p_k"); p_v = bank("p_v"); p_r = bank("p_r")
        p_tok = bank("p_tok"); p_h = [bank("p_h0"), bank("p_h1")]; p_f = bank("p_f")

        names = """x_first x_second x_rest weights_in vecs_in zeroed ident_ready halves ew_ready ew2_ready decay_ready
        ln1_stats ln1_halves ln1_sums ln1_sq ln1_mean ln1_moments ln1_var ln1_rstd z1_ready nm1_ready y1_ready z1_T xn_ready dif_ready
        mixed_ready kvr_done k_done v_done exp_done gate_r ekv_ready num_ready den_ready den_eps rden_ready gated_ready rw_ready
        wo_done x2_ready res_ready ln2_stats ln2_halves ln2_sums ln2_sq ln2_mean ln2_moments ln2_var ln2_rstd z2_ready z2_T yn_ready ysum_ready
        rr_done trr_ready fk_done relu_done kk_ready fv_done ffn_ready x3_ready
        ln3_stats ln3_halves ln3_sums ln3_sq ln3_mean x3_kept ln3_moments ln3_var ln3_rstd xm_ready xm_T xmT_ready scores_done stored
        pads consts scores_in best1 eq1 eqw1 low1 hot1 masked best2 eq2 eqw2 low2 hot2 both_ready gap_ready egap_ready
        esum_ready prob1 prob2 chunk_seen_ready seen_ready rank_done spot_ready spots_ready pos_ready rows_copied ids_in
        dispatched idle_filled pad_filled total_done total_in total_int tiles127 tiles_int tiles_f cum_ready past_ready past_w slot_e_ready
        slot_first_ready slot_start table_w table_row tab1 tab2 w12_in w3_in
        xg_loaded0 xg_loaded1 xg_loaded2 xg_loaded3 xg_T xgT_ready up_done tanh_ready gate_h_ready hid_ready hid_T hidT_ready down_done
        yo_ready scattered0 scattered1 scattered2 scattered3""".split() + [f"o_in{c}" for c in range(CHUNKS)] + ["o_add1", "o_add2"]
        S = {n: sem(n) for n in names}

        def W(n):
            a, b = WOFF[n]
            return w_sb[:, a:b]

        def V(n):
            return vec[:, VEC[n]:VEC[n] + 1]

        def after(eng, name, count):
            if isinstance(count, int) and count <= 0:
                return
            eng.wait_ge(S[name], count)

        def tiles_of(c):
            return bass.ds(c * TPC, TPC)

        block = ctx.enter_context(nc.Block())

        def pipeline(eng, steps, count=CHUNKS, unroll=1, held=1):
            lags = [lag for _, lag in steps]
            first, last = min(lags), count - 1 + max(lags)
            lo, hi = max(lags) + held, count - 1 + min(lags)
            hi -= (hi + 1 - lo) % unroll

            def turn(i, known):
                for step, lag in steps:
                    if not isinstance(i, int) or 0 <= i - lag < count:
                        step(i - lag, (known - lag) % unroll)

            for i in range(first, lo):
                turn(i, i)
            with eng.Fori(lo, hi + 2 - unroll, unroll) as i:
                for u in range(unroll):
                    turn(i + u, lo + u)
            for i in range(hi + 1, last + 1):
                turn(i, i)

        def after_loaded(eng, s, u):
            eng.wait_ge(S[f"xg_loaded{u}"], (s - u) * 4 + 16)

        @block.sync
        def _(sp):
            sp.dma_start(x_all[:, 0:TPC, :], x_in[:, 0:TPC, :]).then_inc(S["x_first"], 16)
            sp.dma_start(x_all[:, TPC:2 * TPC, :], x_in[:, TPC:2 * TPC, :]).then_inc(S["x_second"], 16)
            sp.dma_start(x_all[:, 2 * TPC:, :], x_in[:, 2 * TPC:, :]).then_inc(S["x_rest"], 16)

            def keep(c, _):
                after(sp, "x3_ready", c + 1)
                sp.dma_start(x_all[:, tiles_of(c), :], x3[:, :, :]).then_inc(S["x3_kept"], 16)

            pipeline(sp, [(keep, 0)])

            sp.wait_ge(S["total_int"], 1)
            sp.wait_ge(S["pads"], 3)
            for e in range(E):
                n = sp.value_load(total_i[0:1, e:e + 1], min_val=0, max_val=TOKENS)
                sp.dma_start(rows_d[bass.ds(n + e * REGION, P), :], pad[:, :]).then_inc(S["pad_filled"], 16)
            sp.wait_ge(S["pad_filled"], 16 * E)
            sp.wait_ge(S["idle_filled"], 16)
            sp.wait_ge(S["dispatched"], 16 * TILES * TOPK)
            sp.wait_ge(S["table_row"], 1)

            def load(s, u):
                row = sp.value_load(slot_row[0:1, bass.ds(s, 1)], min_val=0, max_val=E * REGION + (IDLE - 1) * P)
                after(sp, f"scattered{u}", 4 * (s - u))
                sp.dma_start(xg[u][:, :], rows_d[bass.ds(row, P), :]).then_inc(S[f"xg_loaded{u}"], 16)

            pipeline(sp, [(load, 0)], SLOTS, 4, 4)
            for u in range(4):
                sp.wait_ge(S[f"scattered{u}"], 16 * SLOTS // 4)
            res_v = res_d.rearrange("(p t k) d -> p t k d", p=P, k=TOPK)
            for c in range(CHUNKS):
                sp.dma_start(o_all[:, c * TPC:(c + 1) * TPC, :, :], res_v[:, c * TPC:(c + 1) * TPC, :, :])\
                    .then_inc(S[f"o_in{c}"], 16)

        @block.gpsimd
        def _(pool):
            pool.memset(ident[:, :], 0.0).then_inc(S["zeroed"], 1)
            pool.memset(neg_half[:, :], -0.5).then_inc(S["halves"], 1)
            pool.memset(xn[:, :, 0:1], 0.0)
            pool.memset(yn[:, :, 0:1], 0.0).then_inc(S["zeroed"], 1)
            pool.wait_ge(S["zeroed"], 2)
            pool.affine_select(out=ident[:, :], in_=ident[:, :], compare_op=ALU.not_equal, fill=1.0, base=0,
                               pattern=[[-1, P]], channel_multiplier=1).then_inc(S["ident_ready"], 1)
            pool.memset(ones[:, :], 1.0).then_inc(S["consts"], 1)
            pool.memset(tri[:, :], 1.0).then_inc(S["consts"], 1)
            pool.memset(pad[:, :], 0.0).then_inc(S["pads"], 1)
            pool.wait_ge(S["pads"], 1)
            pool.memset(pad[:, D:D + 1].bitcast(I32), NOWHERE).then_inc(S["pads"], 1)
            pool.memset(ones_e[:, :], 1.0).then_inc(S["consts"], 1)
            pool.wait_ge(S["consts"], 2)
            pool.affine_select(out=tri[:, :], in_=tri[:, :], compare_op=ALU.is_gt, fill=0.0, base=0,
                               pattern=[[1, P]], channel_multiplier=-1).then_inc(S["consts"], 1)
            small = dict(channel_multiplier=0, allow_small_or_imprecise_dtypes=True)
            pool.iota(rev[:, :, :], pattern=[[0, TPC], [-1, E]], base=E, **small).then_inc(S["consts"], 1)
            pool.iota(region[:, :, :], pattern=[[0, TPC], [REGION, E]], base=0, **small).then_inc(S["consts"], 1)
            pool.iota(slot_no[:, :], pattern=[[1, SLOTS]], base=0, **small).then_inc(S["consts"], 1)
            pool.iota(ids[:, :, :], pattern=[[TOPK, TILES], [1, TOPK]], base=0, channel_multiplier=TILES * TOPK)\
                .then_inc(S["consts"], 1)
            pool.wait_ge(S["pads"], 2)
            pool.memset(pad[:, D + 1:D + 2], 0.0).then_inc(S["pads"], 1)
            pool.wait_ge(S["halves"], 1)

            def ln1_power(c, _):
                after(pool, "ln1_var", c + 1)
                after(pool, "y1_ready", c)
                pool.tensor_tensor(rs1[:, :], var1[:, :], neg_half[:, :], ALU.pow).then_inc(S["ln1_rstd"], 1)

            def difference(c, _):
                after(pool, "xn_ready", c + 1)
                after(pool, "mixed_ready", c)
                pool.tensor_tensor(dif[:, :, :], xn[:, :, 1:L + 1], xn[:, :, 0:L], ALU.subtract)\
                    .then_inc(S["dif_ready"], 1)

            def ln2_power(c, _):
                after(pool, "ln2_var", c + 1)
                after(pool, "z2_ready", c)
                pool.tensor_tensor(rs2[:, :], var2[:, :], neg_half[:, 0:TPC], ALU.pow).then_inc(S["ln2_rstd"], 1)

            def add_residual(c, _):
                after(pool, "x2_ready", c + 1)
                pool.tensor_tensor(x_all[:, tiles_of(c), :], x_all[:, tiles_of(c), :], x2[:, :, :], ALU.add)\
                    .then_inc(S["res_ready"], 1)

            def shift_sum(c, _):
                after(pool, "yn_ready", c + 1)
                after(pool, "fk_done", FB * c)
                pool.tensor_tensor(ysum[:, :, :], yn[:, :, 1:L + 1], yn[:, :, 0:L], ALU.add)\
                    .then_inc(S["ysum_ready"], 1)

            def squares(c, _):
                after(pool, "fv_done", c)
                for f in range(FB):
                    after(pool, "relu_done", FB * c + f + 1)
                    pool.tensor_tensor(kk[:, f, :], hr[:, f, :], hr[:, f, :], ALU.mult).then_inc(S["kk_ready"], 1)

            def ln3_power(c, _):
                after(pool, "ln3_var", c + 1)
                after(pool, "xm_ready", c)
                pool.tensor_tensor(rs3[:, :], var3[:, :], neg_half[:, 0:TPC], ALU.pow).then_inc(S["ln3_rstd"], 1)

            def dispatch(c, _):
                after(pool, "rows_copied", c + 1)
                after(pool, "ids_in", c + 1)
                after(pool, "prob2", c + 1)
                after(pool, "pos_ready", c + 1)
                for t in range(TPC):
                    for k in range(TOPK):
                        pool.indirect_dma_start(
                            out=rows_d[:, :], out_offset=bass.IndirectOffsetOnAxis(ap=pos[:, k, t:t + 1], axis=0),
                            in_=rows[:, t, k, :], in_offset=None, bounds_check=c + E * REGION, oob_is_err=False)\
                            .then_inc(S["dispatched"], 16)

            pipeline(pool, [(ln1_power, -1), (squares, 1), (difference, -1), (ln2_power, 0), (add_residual, 0),
                            (ln3_power, 1), (shift_sum, 0), (dispatch, 2)])

            def scatter(s, u):
                after(pool, "yo_ready", s + 1)
                pool.indirect_dma_start(
                    out=res_d[:, :], out_offset=bass.IndirectOffsetOnAxis(ap=xg[u][:, D:D + 1].bitcast(U32), axis=0),
                    in_=yo[u][:, :], in_offset=None, bounds_check=s + RESULTS, oob_is_err=False)\
                    .then_inc(S[f"scattered{u}"], 16)

            pipeline(pool, [(scatter, 0)], SLOTS, 4, 4)

        @block.scalar
        def _(act):
            act.dma_start(vec[:, :], v_in).then_inc(S["vecs_in"], 16)
            act.dma_start(w_sb[:, :], w_in).then_inc(S["weights_in"], 16)
            act.dma_start(w12_sb[:, :], w12_in).then_inc(S["w12_in"], 16)
            act.dma_start(w3_sb[:, :], w3_in).then_inc(S["w3_in"], 16)
            act.wait_ge(S["pads"], 3)
            act.dma_start(rows_d[E * REGION:, :].rearrange("(k p) w -> p k w", p=P),
                          pad[:, :].rearrange("p (o w) -> p o w", o=1).to_broadcast([P, IDLE, ROW])).then_inc(S["idle_filled"], 16)
            act.wait_ge(S["vecs_in"], 16)
            act.activation(ew[:, 0:1], V("time_decay"), ACT.Exp).then_inc(S["ew_ready"], 1)
            act.wait_ge(S["ew_ready"], 1)
            act.activation(ew[:, 1:2], ew[:, 0:1], ACT.Exp, scale=-1.0).then_inc(S["ew2_ready"], 1)
            act.wait_ge(S["zeroed"], 2)

            def normed_x(c, _):
                after(act, "z1_T", c + 1)
                after(act, "mixed_ready", c)
                act.activation(xn[:, :, 1:L + 1], p_tr[:, :].rearrange("p (b l) -> p b l", b=BPC), ACT.Identity,
                               bias=V("ln1_b"), scale=V("ln1_g")).then_inc(S["xn_ready"], 1)

            def exps(c, _):
                after(act, "k_done", c + 1)
                after(act, "den_ready", c)
                pk = p_k[:, :].rearrange("p (b l) -> p b l", b=BPC)
                act.activation(ek[:, :, 0:1], pk[:, :, 0:1], ACT.Exp, bias=V("time_first"))
                act.activation(ek[:, :, 1:L], pk[:, :, 1:L], ACT.Exp).then_inc(S["exp_done"], 1)
                after(act, "kvr_done", c + 1)
                after(act, "gated_ready", c)
                act.activation(tr[:, :], p_r[:, :], ACT.Tanh, scale=0.5).then_inc(S["gate_r"], 1)

            def normed_y(c, _):
                after(act, "z2_T", c + 1)
                after(act, "ysum_ready", c)
                after(act, "rr_done", c)
                act.activation(yn[:, :, 1:L + 1], p_tr[:, :].rearrange("p (b l) -> p b l", b=BPC), ACT.Identity,
                               bias=V("ln2_b"), scale=V("ln2_g")).then_inc(S["yn_ready"], 1)

            def relus(c, _):
                after(act, "rr_done", c + 1)
                after(act, "ffn_ready", c)
                act.activation(trr[:, :], p_tok[:, :], ACT.Tanh, scale=0.5).then_inc(S["trr_ready"], 1)
                after(act, "kk_ready", FB * c)
                for f in range(FB):
                    after(act, "fk_done", FB * c + f + 1)
                    act.activation(hr[:, f, :], p_h[f % 2][:, :], ACT.Relu, scale=0.5).then_inc(S["relu_done"], 1)

            def normed_m(c, _):
                after(act, "xm_T", c + 1)
                after(act, "scores_done", c)
                act.activation(xmT[:, :], p_tr[:, :], ACT.Copy).then_inc(S["xmT_ready"], 1)

            def copy_rows(c, _):
                after(act, "xm_ready", c + 1)
                after(act, "dispatched", 16 * TPC * TOPK * c)
                act.activation(rows[:, :, :, 0:D], xm[:, :, :].rearrange("p t (o d) -> p t o d", o=1).to_broadcast([P, TPC, TOPK, D]),
                               ACT.Copy).then_inc(S["rows_copied"], 1)

            def gap_exp(c, _):
                after(act, "gap_ready", c + 1)
                after(act, "prob2", c)
                act.activation(egap[:, :], gap[:, :], ACT.Exp).then_inc(S["egap_ready"], 1)

            pipeline(act, [(exps, 0), (normed_m, 2), (copy_rows, 2), (relus, 1), (gap_exp, 2), (normed_x, -1), (normed_y, 0)])

            def turned_rows(s, u):
                after(act, "xg_T", s + 1)
                after(act, "up_done", s - 1)
                act.activation(xgT[u][:, :], p_tr[:, u * P:(u + 1) * P], ACT.Copy).then_inc(S["xgT_ready"], 1)

            def tanh(s, u):
                after(act, "up_done", s + 1)
                after(act, "gate_h_ready", s - 1)
                act.activation(th[u][:, :], p_h[u][:, 0:H], ACT.Tanh, scale=0.5).then_inc(S["tanh_ready"], 1)

            def turned_hidden(s, u):
                after(act, "hid_T", s + 1)
                after(act, "down_done", s - 1)
                act.activation(hidT[u][:, :, :], p_k[:, 0:2 * P].rearrange("p (j m) -> p j m", j=2), ACT.Copy)\
                    .then_inc(S["hidT_ready"], 1)

            pipeline(act, [(tanh, 0), (turned_hidden, 1), (turned_rows, -1)], SLOTS, 2, 4)
            for c in range(CHUNKS):
                act.wait_ge(S["o_add2"], c + 1)
                act.dma_start(out[:, c * TPC:(c + 1) * TPC, :], x_all[:, c * TPC:(c + 1) * TPC, :]).then_inc(S["stored"], 16)
            act.wait_ge(S["stored"], 16 * CHUNKS)

        @block.tensor
        def _(pe):
            pe.wait_ge(S["ident_ready"], 1)
            pe.wait_ge(S["weights_in"], 16)
            pe.wait_ge(S["consts"], 8)

            def turn_tiles(src, done):
                for t in range(TPC):
                    mm = pe.transpose(p_tr[:, t * P:(t + 1) * P], src[:, t, :], ident[:, :])
                mm.then_inc(S[done], 1)

            def turn_x(c, _):
                after(pe, "z1_ready", c + 1)
                after(pe, "xmT_ready", c - 2)
                after(pe, "yn_ready", c - 1)
                turn_tiles(z1, "z1_T")

            def kvr(c, _):
                after(pe, "mixed_ready", c + 1)
                after(pe, "exp_done", c)
                pe.matmul(p_k[:, :], W("Wk"), mixed[0][:, :, :].rearrange("p b l -> p (b l)"), start=True, stop=True)\
                    .then_inc(S["k_done"], 1)
                after(pe, "ekv_ready", c)
                pe.matmul(p_v[:, :], W("Wv"), mixed[1][:, :, :].rearrange("p b l -> p (b l)"), start=True, stop=True)\
                    .then_inc(S["v_done"], 1)
                after(pe, "gate_r", c)
                pe.matmul(p_r[:, :], W("Wr"), mixed[2][:, :, :].rearrange("p b l -> p (b l)"), start=True, stop=True)\
                    .then_inc(S["kvr_done"], 1)

            def attn_out(c, _):
                after(pe, "rw_ready", c + 1)
                after(pe, "trr_ready", c)
                for t in range(TPC):
                    mm = pe.matmul(p_tok[:, t * P:(t + 1) * P], rw[:, t * P:(t + 1) * P], W("Wo"),
                                   start=True, stop=True)
                mm.then_inc(S["wo_done"], 1)

            def turn_y(c, _):
                after(pe, "z2_ready", c + 1)
                after(pe, "xn_ready", c + 2 if not isinstance(c, int) else min(c + 2, CHUNKS))
                turn_tiles(z2, "z2_T")

            def ffn_in(c, _):
                after(pe, "yn_ready", c + 1)
                after(pe, "x2_ready", c + 1)
                for t in range(TPC):
                    tile = yn[:, t // 2, 1 + (t % 2) * P:1 + (t % 2 + 1) * P]
                    mm = pe.matmul(p_tok[:, t * P:(t + 1) * P], tile, W("Wfr"), start=True, stop=True)
                mm.then_inc(S["rr_done"], 1)
                after(pe, "ysum_ready", c + 1)
                for f in range(FB):
                    after(pe, "relu_done", FB * c + f - 1)
                    pe.matmul(p_h[f % 2][:, :], W("Wfk")[:, f * P:(f + 1) * P],
                              ysum[:, :, :].rearrange("p b l -> p (b l)"), start=True, stop=True)\
                        .then_inc(S["fk_done"], 1)

            def ffn_out(c, _):
                after(pe, "kk_ready", FB * (c + 1))
                after(pe, "ffn_ready", c)
                after(pe, "spot_ready", c)
                for t in range(TPC):
                    for f in range(FB):
                        mm = pe.matmul(p_f[:, t * P:(t + 1) * P], kk[:, f, t * P:(t + 1) * P],
                                       W("Wfv")[:, f * P:(f + 1) * P], start=(f == 0), stop=(f == FB - 1))
                mm.then_inc(S["fv_done"], 1)

            def turn_m(c, _):
                after(pe, "xm_ready", c + 1)
                after(pe, "yn_ready", c + 2 if not isinstance(c, int) else min(c + 2, CHUNKS))
                turn_tiles(xm, "xm_T")

            def scores(c, _):
                after(pe, "xmT_ready", c + 1)
                after(pe, "ffn_ready", c + 1)
                for t in range(TPC):
                    mm = pe.matmul(p_f[:, t * E:(t + 1) * E], xmT[:, t * P:(t + 1) * P], W("gate"), start=True, stop=True)
                mm.then_inc(S["scores_done"], 1)

            def ranks(c, _):
                after(pe, "both_ready", c + 1)
                after(pe, "scores_in", c + 1)
                r = p_f[:, 0:TPC * E].rearrange("p (t e) -> p t e", t=TPC)
                after(pe, "seen_ready", c + 1)
                pe.matmul(r, tri[:, :], both[:, :, :], start=True, stop=False)
                for t in range(TPC - 1):
                    pe.matmul(r[:, t + 1:, :], ones[:, :], both[:, t:t + 1, :].to_broadcast([P, TPC - 1 - t, E]),
                              start=False, stop=False)
                pe.matmul(r, ones[:, :], seen[:, :].rearrange("p (o e) -> p o e", o=1).to_broadcast([P, TPC, E]),
                          start=False, stop=True).then_inc(S["rank_done"], 1)

            pipeline(pe, [(kvr, 0), (turn_m, 2), (scores, 2), (ffn_in, 1), (turn_x, -1), (ranks, 2), (attn_out, 0), (ffn_out, 1), (turn_y, 0)])

            pe.wait_ge(S["seen_ready"], CHUNKS + 1)
            pe.wait_ge(S["spot_ready"], CHUNKS)
            pe.matmul(p_f[:, 0:E], ones[:, :], seen[:, :], start=True, stop=True).then_inc(S["total_done"], 1)

            pe.wait_ge(S["table_w"], 1)
            pe.wait_ge(S["w12_in"], 16)
            pe.wait_ge(S["w3_in"], 16)

            def turn_rows(s, u):
                after_loaded(pe, s, u)
                after(pe, "xgT_ready", s - 1)
                pe.transpose(p_tr[:, (u % 2) * P:(u % 2 + 1) * P], xg[u][:, 0:D], ident[:, :]).then_inc(S["xg_T"], 1)

            def up(s, u):
                w = pe.value_load(slot_w[0:1, bass.ds(s, 1)], min_val=0, max_val=E - 1)
                after(pe, "xgT_ready", s + 1)
                after(pe, "hid_ready", s - 1)
                pe.matmul(p_h[u % 2][:, :], xgT[u % 2][:, :], w12_sb[:, bass.ds(w * (2 * H), 2 * H)], start=True, stop=True)\
                    .then_inc(S["up_done"], 1)

            def turn_hidden(s, u):
                after(pe, "hid_ready", s + 1)
                after(pe, "hidT_ready", s)
                for j in range(2):
                    mm = pe.transpose(p_k[:, j * P:(j + 1) * P], hid[u % 2][:, j * P:(j + 1) * P], ident[:, :])
                mm.then_inc(S["hid_T"], 1)

            def down(s, u):
                w = pe.value_load(slot_w[0:1, bass.ds(s, 1)], min_val=0, max_val=E - 1)
                after(pe, "hidT_ready", s + 1)
                after(pe, "yo_ready", s - 1)
                p_y = (p_v, p_r)[u % 2]
                for j in range(2):
                    mm = pe.matmul(p_y[:, 0:D], hidT[u % 2][:, j, :], w3_sb[:, bass.ds(w * (2 * D) + j * D, D)],
                                   start=(j == 0), stop=(j == 1))
                mm.then_inc(S["down_done"], 1)

            pipeline(pe, [(up, 0), (down, 2), (turn_hidden, 1), (turn_rows, -1)], SLOTS, 4, 4)

        @block.vector
        def _(dve):
            dve.wait_ge(S["ew2_ready"], 1)
            dve.memset(decay[:, :], 0.0).then_inc(S["decay_ready"], 1)
            dve.wait_ge(S["decay_ready"], 1)
            dv = decay[:, :].rearrange("p (b l) -> p b l", b=BPC)
            dve.tensor_scalar(dv[:, :, 1:L], dv[:, :, 1:L], ew[:, 1:2], None, ALU.add).then_inc(S["decay_ready"], 1)
            dve.wait_ge(S["decay_ready"], 2)
            dve.memset(seen[:, :], 0.0).then_inc(S["seen_ready"], 1)
            dve.wait_ge(S["consts"], 8)

            def moments(src, st, mv, dm, which, c):
                for t in range(TPC):
                    last = dve.bn_stats(st[:, t, :], src(t))
                last.then_inc(S[which + "_stats"], 1)
                after(dve, which + "_stats", c + 1)
                dve.tensor_tensor(dm[:, :], st[:, :, 1], st[:, :, 4], ALU.subtract).then_inc(S[which + "_halves"], 1)
                dve.tensor_tensor(mv[:, :, :], st[:, :, 1:3], st[:, :, 4:6], ALU.add).then_inc(S[which + "_sums"], 1)
                after(dve, which + "_halves", c + 1)
                dve.tensor_tensor(dm[:, :], dm[:, :], dm[:, :], ALU.mult).then_inc(S[which + "_sq"], 1)
                after(dve, which + "_sums", c + 1)
                dve.tensor_scalar(mv[:, :, 0], mv[:, :, 0], 0.5, None, ALU.mult).then_inc(S[which + "_mean"], 1)
                after(dve, which + "_sq", c + 1)
                dve.scalar_tensor_tensor(out=mv[:, :, 1], in0=dm[:, :], scalar=D / 4, in1=mv[:, :, 1],
                                         op0=ALU.mult, op1=ALU.add).then_inc(S[which + "_moments"], 1)
                after(dve, which + "_moments", c + 1)

            def ln1(c, _):
                if isinstance(c, int) and c < 2:
                    dve.wait_ge(S["x_first" if c == 0 else "x_second"], 16)
                else:
                    dve.wait_ge(S["x_rest"], 16)
                moments(lambda t: x_all[:, bass.ds(c * TPC + t, 1), :].rearrange("p o d -> p (o d)"), st1, mv1, dm1, "ln1", c)
                after(dve, "ln1_rstd", c)
                v = mv1[:, :, 1]
                dve.tensor_scalar(var1[:, 0:TPC], v, 1.0 / D, LN_EPS, ALU.mult, ALU.add)
                dve.tensor_scalar(var1[:, TPC:], v, (1.0 + LN_EPS) / D, LN_EPS * LN_EPS, ALU.mult, ALU.add)\
                    .then_inc(S["ln1_var"], 1)

            def ln1_apply(c, _):
                after(dve, "ln1_rstd", c + 1)
                after(dve, "z1_T", c)
                for t in range(TPC):
                    xt = x_all[:, bass.ds(c * TPC + t, 1), :].rearrange("p o d -> p (o d)")
                    last = dve.tensor_scalar(z1[:, t, :], xt, mv1[:, t, 0:1], rs1[:, TPC + t:TPC + t + 1],
                                             ALU.subtract, ALU.mult)
                last.then_inc(S["z1_ready"], 1)

            def first_norm(c, _):
                for t in range(TPC):
                    xt = x_all[:, bass.ds(c * TPC + t, 1), :].rearrange("p o d -> p (o d)")
                    last = dve.tensor_scalar(y1[:, t, :], xt, mv1[:, t, 0:1], rs1[:, t:t + 1],
                                             ALU.subtract, ALU.mult)
                last.then_inc(S["y1_ready"], 1)

            def mixes(c, _):
                after(dve, "dif_ready", c + 1)
                after(dve, "kvr_done", c)
                for n, m in enumerate(["mix_k", "mix_v", "mix_r"]):
                    last = dve.scalar_tensor_tensor(out=mixed[n][:, :, :], in0=dif[:, :, :], scalar=V(m),
                                                    in1=xn[:, :, 0:L], op0=ALU.mult, op1=ALU.add)
                last.then_inc(S["mixed_ready"], 1)

            def wkv(c, _):
                after(dve, "exp_done", c + 1)
                after(dve, "v_done", c + 1)
                ekf = ek[:, :, :].rearrange("p b l -> p (b l)")
                dve.tensor_tensor(ekv[:, :], ekf, p_v[:, :], ALU.mult).then_inc(S["ekv_ready"], 1)
                dve.tensor_tensor_scan(den[:, :], decay[:, :], ekf, 0.0, ALU.mult, ALU.add).then_inc(S["den_ready"], 1)
                after(dve, "den_ready", c + 1)
                dve.tensor_scalar(den[:, :], den[:, :], WKV_EPS, None, ALU.add).then_inc(S["den_eps"], 1)
                after(dve, "ekv_ready", c + 1)
                dve.tensor_tensor_scan(num[:, :], decay[:, :], ekv[:, :], 0.0, ALU.mult, ALU.add)\
                    .then_inc(S["num_ready"], 1)
                after(dve, "den_eps", c + 1)
                dve.reciprocal(rden[:, :], den[:, :]).then_inc(S["rden_ready"], 1)
                after(dve, "gate_r", c + 1)
                after(dve, "num_ready", c + 1)
                dve.scalar_tensor_tensor(out=gated[:, :], in0=tr[:, :], scalar=1.0, in1=num[:, :],
                                         op0=ALU.add, op1=ALU.mult).then_inc(S["gated_ready"], 1)
                after(dve, "gated_ready", c + 1)
                after(dve, "rden_ready", c + 1)
                after(dve, "wo_done", c)
                dve.tensor_tensor(rw[:, :], gated[:, :], rden[:, :], ALU.mult).then_inc(S["rw_ready"], 1)

            def ln2(c, _):
                after(dve, "wo_done", c + 1)
                after(dve, "y1_ready", c + 1)
                after(dve, "res_ready", c)
                dve.scalar_tensor_tensor(out=x2[:, :, :], in0=p_tok[:, :].rearrange("p (t d) -> p t d", t=TPC),
                                         scalar=0.5, in1=y1[:, :, :], op0=ALU.mult, op1=ALU.add)\
                    .then_inc(S["x2_ready"], 1)
                after(dve, "x2_ready", c + 1)
                moments(lambda t: x2[:, t, :], st2, mv2, dm2, "ln2", c)
                after(dve, "ln2_rstd", c)
                dve.tensor_scalar(var2[:, :], mv2[:, :, 1], 1.0 / D, LN_EPS, ALU.mult, ALU.add).then_inc(S["ln2_var"], 1)

            def ln2_apply(c, _):
                after(dve, "ln2_rstd", c + 1)
                after(dve, "z2_T", c)
                for t in range(TPC):
                    last = dve.tensor_scalar(z2[:, t, :], x2[:, t, :], mv2[:, t, 0:1], rs2[:, t:t + 1],
                                             ALU.subtract, ALU.mult)
                last.then_inc(S["z2_ready"], 1)

            def ln3(c, _):
                after(dve, "fv_done", c + 1)
                after(dve, "trr_ready", c + 1)
                dve.scalar_tensor_tensor(out=ffn[:, :], in0=trr[:, :], scalar=1.0, in1=p_f[:, :],
                                         op0=ALU.add, op1=ALU.mult).then_inc(S["ffn_ready"], 1)
                after(dve, "ffn_ready", c + 1)
                after(dve, "res_ready", c + 1)
                after(dve, "x3_kept", 16 * c)
                dve.scalar_tensor_tensor(out=x3[:, :, :], in0=ffn[:, :].rearrange("p (t d) -> p t d", t=TPC),
                                         scalar=0.5, in1=x_all[:, tiles_of(c), :], op0=ALU.mult, op1=ALU.add)\
                    .then_inc(S["x3_ready"], 1)
                after(dve, "x3_ready", c + 1)
                moments(lambda t: x3[:, t, :], st3, mv3, dm3, "ln3", c)
                after(dve, "ln3_rstd", c)
                dve.tensor_scalar(var3[:, :], mv3[:, :, 1], 1.0 / D, LN_EPS, ALU.mult, ALU.add).then_inc(S["ln3_var"], 1)

            def ln3_apply(c, _):
                after(dve, "ln3_rstd", c + 1)
                after(dve, "xm_T", c)
                for t in range(TPC):
                    last = dve.tensor_scalar(xm[:, t, :], x3[:, t, :], mv3[:, t, 0:1], rs3[:, t:t + 1],
                                             ALU.subtract, ALU.mult)
                last.then_inc(S["xm_ready"], 1)

            def flat(ap, o):
                return ap.rearrange("p (t o) -> p t o", o=1).to_broadcast([P, TPC, E])

            def pick_one(c, k):
                n = str(k + 1)
                dve.tensor_reduce(best[:, k, :], sc[:, :, :], mybir.AxisListType.X, ALU.max).then_inc(S["best" + n], 1)
                after(dve, "best" + n, c + 1)
                dve.tensor_tensor(eq[:, :, :], sc[:, :, :], flat(best[:, k, :], E), ALU.is_equal).then_inc(S["eq" + n], 1)
                after(dve, "eq" + n, c + 1)
                dve.tensor_tensor(eq[:, :, :], eq[:, :, :], rev[:, :, :], ALU.mult).then_inc(S["eqw" + n], 1)
                after(dve, "eqw" + n, c + 1)
                dve.tensor_reduce(low[:, :], eq[:, :, :], mybir.AxisListType.X, ALU.max).then_inc(S["low" + n], 1)
                after(dve, "low" + n, c + 1)
                dve.tensor_tensor(hot[:, k, :, :], rev[:, :, :], flat(low[:, :], E), ALU.is_equal).then_inc(S["hot" + n], 1)
                after(dve, "hot" + n, c + 1)

            def pick(c, _):
                after(dve, "scores_done", c + 1)
                dve.tensor_copy(sc[:, :, :], p_f[:, 0:TPC * E].rearrange("p (t e) -> p t e", t=TPC)).then_inc(S["scores_in"], 1)
                after(dve, "scores_in", c + 1)
                pick_one(c, 0)
                dve.scalar_tensor_tensor(out=sc[:, :, :], in0=hot[:, 0, :, :], scalar=-3.0e38, in1=sc[:, :, :],
                                         op0=ALU.mult, op1=ALU.add).then_inc(S["masked"], 1)
                after(dve, "masked", c + 1)
                pick_one(c, 1)
                after(dve, "rank_done", c)
                dve.tensor_tensor(both[:, :, :], hot[:, 0, :, :], hot[:, 1, :, :], ALU.add).then_inc(S["both_ready"], 1)
                dve.tensor_tensor(gap[:, :], best[:, 1, :], best[:, 0, :], ALU.subtract).then_inc(S["gap_ready"], 1)

            def place(c, _):
                after(dve, "egap_ready", c + 1)
                dve.tensor_scalar(esum[:, :], egap[:, :], 1.0, None, ALU.add).then_inc(S["esum_ready"], 1)
                after(dve, "dispatched", 16 * TPC * TOPK * c)
                dve.tensor_copy(rows[:, :, :, D:D + 1].bitcast(I32),
                                ids[:, tiles_of(c), :].rearrange("p t (k o) -> p t k o", o=1)).then_inc(S["ids_in"], 1)
                after(dve, "esum_ready", c + 1)
                dve.reciprocal(prob[:, :, 0], esum[:, :]).then_inc(S["prob1"], 1)
                after(dve, "prob1", c + 1)
                dve.tensor_copy(rows[:, :, 0, D + 1], prob[:, :, 0])
                dve.tensor_tensor(rows[:, :, 1, D + 1], prob[:, :, 0], egap[:, :], ALU.mult).then_inc(S["prob2"], 1)
                after(dve, "rank_done", c + 1)
                dve.tensor_tensor(spot[:, :, :], region[:, :, :], p_f[:, 0:TPC * E].rearrange("p (t e) -> p t e", t=TPC),
                                  ALU.add).then_inc(S["spot_ready"], 1)
                dve.tensor_reduce(chunk_seen[:, :], both[:, :, :].rearrange("p t e -> p e t"), mybir.AxisListType.X,
                                  ALU.add).then_inc(S["chunk_seen_ready"], 1)
                after(dve, "spot_ready", c + 1)
                for k in range(TOPK):
                    last = dve.tensor_tensor(spots[:, k, :, :], hot[:, k, :, :], spot[:, :, :], ALU.mult)
                last.then_inc(S["spots_ready"], 1)
                after(dve, "chunk_seen_ready", c + 1)
                dve.tensor_tensor(seen[:, :], seen[:, :], chunk_seen[:, :], ALU.add).then_inc(S["seen_ready"], 1)
                after(dve, "spots_ready", c + 1)
                with nc.allow_low_precision(reason="whole numbers under 2**24, summed in float32"):
                    dve.tensor_reduce(pos[:, :, :], spots[:, :, :, :], mybir.AxisListType.X, ALU.add)\
                        .then_inc(S["pos_ready"], 1)

            pipeline(dve, [(ln1, -1), (pick, 2), (wkv, 0), (ln1_apply, -1), (place, 2), (ln2, 0), (first_norm, -1), (mixes, -1),
                           (ln2_apply, 0), (ln3, 1), (ln3_apply, 1)])

            def link(ins, name):
                ins.then_inc(S[name], 1)
                dve.wait_ge(S[name], 1)

            dve.wait_ge(S["total_done"], 1)
            link(dve.tensor_copy(total[:, :], p_f[:, 0:E]), "total_in")
            dve.tensor_copy(total_i[:, :], total[:, :]).then_inc(S["total_int"], 1)
            link(dve.tensor_scalar(ntile_i[:, :], total[:, :], float(P - 1), None, ALU.add), "tiles127")
            link(dve.tensor_scalar(ntile_i[:, :], ntile_i[:, :], P.bit_length() - 1, None, ALU.arith_shift_right), "tiles_int")
            link(dve.tensor_copy(ntile[:, :], ntile_i[:, :]), "tiles_f")
            link(dve.tensor_tensor_scan(cum[:, :], ones_e[:, :], ntile[:, :], 0.0, ALU.mult, ALU.add), "cum_ready")
            over_e = lambda ap: ap.rearrange("p (s o) -> p s o", o=1).to_broadcast([P, SLOTS, E])
            over_s = lambda ap: ap.rearrange("p (o e) -> p o e", o=1).to_broadcast([P, SLOTS, E])
            link(dve.tensor_tensor(past[:, :, :], over_e(slot_no[:, :]), over_s(cum[:, :]), ALU.is_ge), "past_ready")
            link(dve.tensor_reduce(slot_e[:, :], past[:, :, :], mybir.AxisListType.X, ALU.add), "slot_e_ready")
            dve.tensor_scalar(slot_w[:, :], slot_e[:, :], float(E - 1), None, ALU.min).then_inc(S["table_w"], 1)
            link(dve.tensor_tensor(past_tiles[:, :, :], past[:, :, :], over_s(ntile[:, :]), ALU.mult), "past_w")
            link(dve.tensor_reduce(slot_first[:, :], past_tiles[:, :, :], mybir.AxisListType.X, ALU.add), "slot_first_ready")
            link(dve.tensor_tensor(slot_first[:, :], slot_no[:, :], slot_first[:, :], ALU.subtract), "slot_start")
            link(dve.tensor_scalar(slot_first[:, :], slot_first[:, :], float(P), None, ALU.mult), "tab1")
            dve.scalar_tensor_tensor(out=slot_row[:, :], in0=slot_e[:, :], scalar=float(REGION), in1=slot_first[:, :],
                                     op0=ALU.mult, op1=ALU.add).then_inc(S["table_row"], 1)

            def gate_hidden(s, u):
                after(dve, "tanh_ready", s + 1)
                after(dve, "hid_ready", s)
                dve.scalar_tensor_tensor(out=gate_h[:, :], in0=th[u % 2][:, :], scalar=1.0, in1=p_h[u % 2][:, 0:H],
                                         op0=ALU.add, op1=ALU.mult).then_inc(S["gate_h_ready"], 1)
                after(dve, "gate_h_ready", s + 1)
                after(dve, "hid_T", s - 1)
                dve.tensor_tensor(hid[u % 2][:, :], gate_h[:, :], p_h[u % 2][:, H:2 * H], ALU.mult).then_inc(S["hid_ready"], 1)

            def weigh(s, u):
                after(dve, "down_done", s + 1)
                after(dve, f"scattered{u}", 4 * (s - u))
                p_y = (p_v, p_r)[u % 2]
                dve.tensor_scalar(yo[u][:, :], p_y[:, 0:D], xg[u][:, D + 1:D + 2], 0.5, ALU.mult, ALU.mult)\
                    .then_inc(S["yo_ready"], 1)

            pipeline(dve, [(gate_hidden, 0), (weigh, 2)], SLOTS, 4, 4)

            for c in range(CHUNKS):
                dve.wait_ge(S[f"o_in{c}"], 16)
                dve.wait_ge(S["x3_kept"], 16 * CHUNKS)
                part = slice(c * TPC, (c + 1) * TPC)
                dve.tensor_tensor(x_all[:, part, :], x_all[:, part, :], o_all[:, part, 0, :], ALU.add).then_inc(S["o_add1"], 1)
                dve.wait_ge(S["o_add1"], c + 1)
                dve.tensor_tensor(x_all[:, part, :], x_all[:, part, :], o_all[:, part, 1, :], ALU.add).then_inc(S["o_add2"], 1)


def kernel(**inputs):
    import numpy as np
    import concourse.bacc as bacc
    from concourse.bass_utils import run_bass_kernel_spmd as run

    a = {k.replace("L0_attn_", "").replace("L0_ffn_", ""): np.asarray(v) for k, v in inputs.items()}
    arrays = {
        "x": a["x"].reshape(TILES, P, D).transpose(1, 0, 2),
        "weights": np.concatenate([a["Wk"], a["Wv"], a["Wr"], a["Wo"], a["Wfr"], a["Wfk"],
                                   a["Wfv"].reshape(FB, P, D).transpose(1, 0, 2).reshape(P, FFN),
                                   a["gate_w"].T], axis=1),
        "vecs": np.stack([a[n] for n in VEC], axis=1),
        "w12": a["w12"].transpose(2, 0, 1).reshape(P, E * 2 * H),
        "w3": a["w3"].transpose(2, 0, 1).reshape(2, P, E, D).transpose(1, 2, 0, 3).reshape(P, E * 2 * D),
    }
    arrays = {k: np.ascontiguousarray(v) for k, v in arrays.items()}
    nc = bacc.Bacc("TRN2", target_bir_lowering=False, num_devices=1)
    args = [nc.dram_tensor(k, v.shape, F32, kind="ExternalInput").ap() for k, v in arrays.items()]
    args.append(nc.dram_tensor("out", [P, TILES, D], F32, kind="ExternalOutput").ap())
    build(nc, *args)
    r = run(nc, [arrays], core_ids=[0])
    return r.results[0]["out"].transpose(1, 0, 2).reshape(B, L, D)
```

```python
import concourse.bass as bass
from concourse import mybir
from concourse.alu_op_type import AluOpType as ALU
from contextlib import ExitStack

F32 = mybir.dt.float32
I32 = mybir.dt.int32
U32 = mybir.dt.uint32
ACT = mybir.ActivationFunctionType

B, L, D = 16, 256, 128
P = 128
TOKENS = B * L
TILES = TOKENS // P
TPC = 4
CT = TPC * P
BPC = CT // L
CHUNKS = TILES // TPC
FFN = 4 * D
FB = FFN // P
E, H = 8, 256
LN_EPS = 1e-5
WKV_EPS = 1e-8
VEC = {n: i for i, n in enumerate(
    ["ln1_g", "ln1_b", "mix_k", "mix_v", "mix_r", "ln2_g", "ln2_b", "time_decay", "time_first"])}
WOFF = {}
_at = 0
for _n, _w in [("Wk", D), ("Wv", D), ("Wr", D), ("Wo", D), ("Wfr", D), ("Wfk", FFN), ("Wfv", FFN), ("gate", E)]:
    WOFF[_n] = (_at, _at + _w)
    _at += _w
WCOLS = _at
TOPK = 2
ROW = D + 2
REGION = TOKENS + P
SLOTS = TOKENS * TOPK // P + E
IDLE = E
RESULTS = TOKENS * TOPK
BUFS = 8
NOWHERE = 2 * RESULTS


def build(nc, x_in, w_in, v_in, w12_in, w3_in, out):
    ctx = ExitStack()
    with ctx:
        def sb(name, shape, dt=F32):
            return ctx.enter_context(nc.sbuf_tensor(name, shape, dt))

        def bank(name):
            return ctx.enter_context(nc.psum_tensor(name, [P, CT], F32))

        def sem(name):
            return ctx.enter_context(nc.semaphore(name))

        x_all = sb("x_all", [P, TILES, D])
        w_sb = sb("w_sb", [P, WCOLS])
        vec = sb("vec", [P, len(VEC)])
        ident = sb("ident", [P, P])
        decay = sb("decay", [P, CT])
        ew = sb("ew", [P, 2])
        neg_half = sb("neg_half", [P, 2 * TPC])

        st1 = sb("st1", [P, TPC, 6]); mv1 = sb("mv1", [P, TPC, 2]); dm1 = sb("dm1", [P, TPC])
        st2 = sb("st2", [P, TPC, 6]); mv2 = sb("mv2", [P, TPC, 2]); dm2 = sb("dm2", [P, TPC])
        st3 = sb("st3", [P, TPC, 6]); mv3 = sb("mv3", [P, TPC, 2]); dm3 = sb("dm3", [P, TPC])
        var1 = sb("var1", [P, 2 * TPC]); rs1 = sb("rs1", [P, 2 * TPC])
        var2 = sb("var2", [P, TPC]); rs2 = sb("rs2", [P, TPC])
        var3 = sb("var3", [P, TPC]); rs3 = sb("rs3", [P, TPC])
        nm1 = sb("nm1", [P, 2, TPC]); nm2 = sb("nm2", [P, TPC]); held = sb("held", [P, 1]); held2 = sb("held2", [P, 1])
        z1 = sb("z1", [P, TPC, D]); y1 = sb("y1", [P, TPC, D])
        xn = sb("xn", [P, BPC, L + 1]); dif = sb("dif", [P, BPC, L])
        mixed = [sb(f"mixed_{n}", [P, BPC, L]) for n in "kvr"]
        ek = sb("ek", [P, BPC, L]); ekv = sb("ekv", [P, CT])
        tr = sb("tr", [P, CT]); num = sb("num", [P, CT]); den = sb("den", [P, CT])
        rden = sb("rden", [P, CT]); gated = sb("gated", [P, CT]); rw = sb("rw", [P, CT])
        x2 = sb("x2", [P, TPC, D]); z2 = sb("z2", [P, TPC, D])
        yn = sb("yn", [P, BPC, L + 1]); ysum = sb("ysum", [P, BPC, L])
        trr = sb("trr", [P, CT]); hr = sb("hr", [P, FB, CT]); kk = sb("kk", [P, FB, CT])
        ffn = sb("ffn", [P, CT]); x3 = sb("x3", [P, TPC, D]); xm = sb("xm", [P, TPC, D]); xmT = sb("xmT", [P, CT])

        rows = sb("rows", [P, TPC, TOPK, ROW])
        pad = sb("pad", [P, ROW])
        tri = sb("tri", [P, P]); ones = sb("ones", [P, P])
        rev = sb("rev", [P, TPC, E]); region = sb("region", [P, TPC, E]); ids = sb("ids", [P, TILES, TOPK], I32)
        sc = sb("sc", [P, TPC, E]); eq = sb("eq", [P, TPC, E]); low = sb("low", [P, TPC])
        best = sb("best", [P, TOPK, TPC]); hot = sb("hot", [P, TOPK, TPC, E]); both = sb("both", [P, TPC, E])
        gap = sb("gap", [P, TPC]); egap = sb("egap", [P, TPC]); esum = sb("esum", [P, TPC]); prob = sb("prob", [P, TPC, TOPK])
        seen = sb("seen", [P, E]); chunk_seen = sb("chunk_seen", [P, E])
        spot = sb("spot", [P, TPC, E]); spots = sb("spots", [P, TOPK, TPC, E]); pos = sb("pos", [P, TOPK, TPC], U32)
        total = sb("total", [P, E]); total_i = sb("total_i", [P, E], I32)
        ntile_i = sb("ntile_i", [P, E], I32); ntile = sb("ntile", [P, E]); cum = sb("cum", [P, E])
        ones_e = sb("ones_e", [P, E]); slot_no = sb("slot_no", [P, SLOTS])
        past = sb("past", [P, SLOTS, E]); past_tiles = sb("past_tiles", [P, SLOTS, E])
        slot_e = sb("slot_e", [P, SLOTS]); slot_first = sb("slot_first", [P, SLOTS])
        slot_row = sb("slot_row", [P, SLOTS], I32); slot_w = sb("slot_w", [P, SLOTS], I32)
        w12_sb = sb("w12_sb", [P, E * 2 * H]); w3_sb = sb("w3_sb", [P, E * 2 * D])
        xg = [sb(f"xg{n}", [P, ROW]) for n in range(BUFS)]
        xgT = [sb(f"xgT{n}", [P, P]) for n in range(2)]
        th = [sb(f"th{n}", [P, H]) for n in range(2)]
        gate_h = sb("gate_h", [P, H]); hid = [sb(f"hid{n}", [P, H]) for n in range(2)]
        hidT = [sb(f"hidT{n}", [P, 2, P]) for n in range(2)]
        yo = [sb(f"yo{n}", [P, D]) for n in range(BUFS)]
        o_all = sb("o_all", [P, TILES, TOPK, D])

        rows_d = nc.dram_tensor("rows_d", [E * REGION + IDLE * P, ROW], F32, kind="Internal").ap()
        res_d = nc.dram_tensor("res_d", [RESULTS, D], F32, kind="Internal").ap()

        p_tr = bank("p_tr"); p_k = bank("p_k"); p_v = bank("p_v"); p_r = bank("p_r")
        p_tok = bank("p_tok"); p_h = [bank("p_h0"), bank("p_h1")]; p_f = bank("p_f")

        names = """x_first x_second x_rest weights_in vecs_in zeroed ident_ready halves ew_ready ew2_ready decay_ready
        ln1_stats ln1_halves ln1_sums ln1_sq ln1_mean ln1_moments ln1_var ln1_rstd z1_ready nm1_ready nm2_ready y1_ready z1_T xn_ready dif_ready
        mixed_ready kvr_done k_done v_done exp_done gate_r ekv_ready num_ready den_ready den_eps rden_ready gated_ready rw_ready
        wo_done x2_ready res_ready ln2_stats ln2_halves ln2_sums ln2_sq ln2_mean ln2_moments ln2_var ln2_rstd z2_ready z2_T yn_ready ysum_ready
        rr_done trr_ready fk_done relu_done kk_ready fv_done ffn_ready x3_ready
        ln3_stats ln3_halves ln3_sums ln3_sq ln3_mean x3_kept ln3_moments ln3_var ln3_rstd xm_ready xm_T xmT_ready scores_done stored
        pads consts scores_in picking both_ready gap_ready egap_ready
        esum_ready prob1 prob2 chunk_seen_ready seen_ready rank_done spot_ready spots_ready pos_ready rows_copied ids_in
        dispatched idle_filled pad_filled total_done total_int table_steps table_w table_row act_held act_held2 w12_in w3_in
        xg_T xgT_ready up_done tanh_ready gate_h_ready hid_ready hid_T hidT_ready down_done
        yo_ready""".split() + [f"o_in{c}" for c in range(CHUNKS)] + ["o_add1", "o_add2"]
        names += [f"{n}{b}" for n in ("xg_loaded", "scattered") for b in range(BUFS)]
        S = {n: sem(n) for n in names}

        def W(n):
            a, b = WOFF[n]
            return w_sb[:, a:b]

        def V(n):
            return vec[:, VEC[n]:VEC[n] + 1]

        def after(eng, name, count):
            if isinstance(count, int) and count <= 0:
                return
            eng.wait_ge(S[name], count)

        def tiles_of(c):
            return bass.ds(c * TPC, TPC)

        block = ctx.enter_context(nc.Block())

        def pipeline(eng, steps, count=CHUNKS, unroll=1, held=1):
            lags = [lag for _, lag in steps]
            first, last = min(lags), count - 1 + max(lags)
            lo, hi = max(lags) + held, count - 1 + min(lags)
            hi -= (hi + 1 - lo) % unroll

            def turn(i, known):
                for step, lag in steps:
                    if not isinstance(i, int) or 0 <= i - lag < count:
                        step(i - lag, (known - lag) % unroll)

            for i in range(first, lo):
                turn(i, i)
            with eng.Fori(lo, hi + 2 - unroll, unroll) as i:
                for u in range(unroll):
                    turn(i + u, lo + u)
            for i in range(hi + 1, last + 1):
                turn(i, i)

        def after_loaded(eng, s, u):
            eng.wait_ge(S[f"xg_loaded{u}"], 16 // BUFS * (s - u) + 16)

        @block.sync
        def _(sp):
            sp.dma_start(x_all[:, 0:TPC, :], x_in[:, 0:TPC, :]).then_inc(S["x_first"], 16)
            sp.dma_start(x_all[:, TPC:2 * TPC, :], x_in[:, TPC:2 * TPC, :]).then_inc(S["x_second"], 16)
            sp.dma_start(x_all[:, 2 * TPC:, :], x_in[:, 2 * TPC:, :]).then_inc(S["x_rest"], 16)

            def keep(c, _):
                after(sp, "x3_ready", c + 1)
                sp.dma_start(x_all[:, tiles_of(c), :], x3[:, :, :]).then_inc(S["x3_kept"], 16)

            pipeline(sp, [(keep, 0)])

            sp.wait_ge(S["total_int"], 1)
            sp.wait_ge(S["pads"], 3)
            for e in range(E):
                n = sp.value_load(total_i[0:1, e:e + 1], min_val=0, max_val=TOKENS)
                sp.dma_start(rows_d[bass.ds(n + e * REGION, P), :], pad[:, :]).then_inc(S["pad_filled"], 16)
            sp.wait_ge(S["pad_filled"], 16 * E)
            sp.wait_ge(S["idle_filled"], 16)
            sp.wait_ge(S["dispatched"], 16 * TILES * TOPK)
            sp.wait_ge(S["table_row"], 1)

            def load(s, u):
                row = sp.value_load(slot_row[0:1, bass.ds(s, 1)], min_val=0, max_val=E * REGION + (IDLE - 1) * P)
                after(sp, f"scattered{u}", 16 // BUFS * (s - u))
                sp.dma_start(xg[u][:, :], rows_d[bass.ds(row, P), :]).then_inc(S[f"xg_loaded{u}"], 16)

            pipeline(sp, [(load, 0)], SLOTS, BUFS, BUFS)
            for u in range(BUFS):
                sp.wait_ge(S[f"scattered{u}"], 16 * SLOTS // BUFS)
            res_v = res_d.rearrange("(p t k) d -> p t k d", p=P, k=TOPK)
            for c in range(CHUNKS):
                sp.dma_start(o_all[:, c * TPC:(c + 1) * TPC, :, :], res_v[:, c * TPC:(c + 1) * TPC, :, :])\
                    .then_inc(S[f"o_in{c}"], 16)

        @block.gpsimd
        def _(pool):
            pool.memset(ident[:, :], 0.0).then_inc(S["zeroed"], 1)
            pool.memset(neg_half[:, :], -0.5).then_inc(S["halves"], 1)
            pool.memset(xn[:, :, 0:1], 0.0)
            pool.memset(yn[:, :, 0:1], 0.0).then_inc(S["zeroed"], 1)
            pool.wait_ge(S["zeroed"], 2)
            pool.affine_select(out=ident[:, :], in_=ident[:, :], compare_op=ALU.not_equal, fill=1.0, base=0,
                               pattern=[[-1, P]], channel_multiplier=1).then_inc(S["ident_ready"], 1)
            pool.memset(ones[:, :], 1.0).then_inc(S["consts"], 1)
            pool.memset(tri[:, :], 1.0).then_inc(S["consts"], 1)
            pool.memset(pad[:, :], 0.0).then_inc(S["pads"], 1)
            pool.wait_ge(S["pads"], 1)
            pool.memset(pad[:, D:D + 1].bitcast(I32), NOWHERE).then_inc(S["pads"], 1)
            pool.memset(ones_e[:, :], 1.0).then_inc(S["consts"], 1)
            pool.wait_ge(S["consts"], 2)
            pool.affine_select(out=tri[:, :], in_=tri[:, :], compare_op=ALU.is_gt, fill=0.0, base=0,
                               pattern=[[1, P]], channel_multiplier=-1).then_inc(S["consts"], 1)
            small = dict(channel_multiplier=0, allow_small_or_imprecise_dtypes=True)
            pool.iota(rev[:, :, :], pattern=[[0, TPC], [-1, E]], base=E, **small).then_inc(S["consts"], 1)
            pool.iota(region[:, :, :], pattern=[[0, TPC], [REGION, E]], base=0, **small).then_inc(S["consts"], 1)
            pool.iota(slot_no[:, :], pattern=[[1, SLOTS]], base=0, **small).then_inc(S["consts"], 1)
            pool.iota(ids[:, :, :], pattern=[[TOPK, TILES], [1, TOPK]], base=0, channel_multiplier=TILES * TOPK)\
                .then_inc(S["consts"], 1)
            pool.wait_ge(S["pads"], 2)
            pool.memset(pad[:, D + 1:D + 2], 0.0).then_inc(S["pads"], 1)
            pool.wait_ge(S["halves"], 1)

            def ln1_power(c, _):
                after(pool, "ln1_var", c + 1)
                after(pool, "y1_ready", c)
                after(pool, "z1_ready", c)
                pool.tensor_tensor(rs1[:, :], var1[:, :], neg_half[:, :], ALU.pow).then_inc(S["ln1_rstd"], 1)
                after(pool, "ln1_rstd", c + 1)
                pool.tensor_tensor(nm1[:, :, :], rs1[:, :].rearrange("p (k t) -> p k t", k=2),
                                   mv1[:, :, 0:1].rearrange("p t o -> p o t").to_broadcast([P, 2, TPC]), ALU.mult)\
                    .then_inc(S["nm1_ready"], 1)

            def difference(c, _):
                after(pool, "xn_ready", c + 1)
                after(pool, "mixed_ready", c)
                pool.tensor_tensor(dif[:, :, :], xn[:, :, 1:L + 1], xn[:, :, 0:L], ALU.subtract)\
                    .then_inc(S["dif_ready"], 1)

            def ln2_power(c, _):
                after(pool, "ln2_var", c + 1)
                after(pool, "z2_ready", c)
                pool.tensor_tensor(rs2[:, :], var2[:, :], neg_half[:, 0:TPC], ALU.pow).then_inc(S["ln2_rstd"], 1)
                after(pool, "ln2_rstd", c + 1)
                pool.tensor_tensor(nm2[:, :], rs2[:, :], mv2[:, :, 0], ALU.mult).then_inc(S["nm2_ready"], 1)

            def add_residual(c, _):
                after(pool, "x2_ready", c + 1)
                pool.tensor_tensor(x_all[:, tiles_of(c), :], x_all[:, tiles_of(c), :], x2[:, :, :], ALU.add)\
                    .then_inc(S["res_ready"], 1)

            def shift_sum(c, _):
                after(pool, "yn_ready", c + 1)
                after(pool, "fk_done", FB * c)
                pool.tensor_tensor(ysum[:, :, :], yn[:, :, 1:L + 1], yn[:, :, 0:L], ALU.add)\
                    .then_inc(S["ysum_ready"], 1)

            def ln3_power(c, _):
                after(pool, "ln3_var", c + 1)
                after(pool, "xm_ready", c)
                pool.tensor_tensor(rs3[:, :], var3[:, :], neg_half[:, 0:TPC], ALU.pow).then_inc(S["ln3_rstd"], 1)

            def dispatch(c, tiles):
                if 0 in tiles:
                    after(pool, "rows_copied", c + 1)
                    after(pool, "ids_in", c + 1)
                    after(pool, "prob2", c + 1)
                    after(pool, "pos_ready", c + 1)
                for t in tiles:
                    for k in range(TOPK):
                        pool.indirect_dma_start(
                            out=rows_d[:, :], out_offset=bass.IndirectOffsetOnAxis(ap=pos[:, k, t:t + 1], axis=0),
                            in_=rows[:, t, k, :], in_offset=None, bounds_check=c + E * REGION, oob_is_err=False)\
                            .then_inc(S["dispatched"], 16)

            pipeline(pool, [(shift_sum, 1), (ln1_power, -1), (lambda c, _: dispatch(c, [0, 1]), 3), (difference, -1),
                            (lambda c, _: dispatch(c, [2, 3]), 3), (ln3_power, 1), (ln2_power, 0), (add_residual, 0)])

            def scatter(s, u):
                after(pool, "yo_ready", s + 1)
                pool.indirect_dma_start(
                    out=res_d[:, :], out_offset=bass.IndirectOffsetOnAxis(ap=xg[u][:, D:D + 1].bitcast(U32), axis=0),
                    in_=yo[u][:, :], in_offset=None, bounds_check=s + RESULTS, oob_is_err=False)\
                    .then_inc(S[f"scattered{u}"], 16)

            pipeline(pool, [(scatter, 0)], SLOTS, BUFS, BUFS)

        @block.scalar
        def _(act):
            act.dma_start(vec[:, :], v_in).then_inc(S["vecs_in"], 16)
            act.dma_start(w_sb[:, :], w_in).then_inc(S["weights_in"], 16)
            act.dma_start(w12_sb[:, :], w12_in).then_inc(S["w12_in"], 16)
            act.dma_start(w3_sb[:, :], w3_in).then_inc(S["w3_in"], 16)
            act.wait_ge(S["pads"], 3)
            act.dma_start(rows_d[E * REGION:, :].rearrange("(k p) w -> p k w", p=P),
                          pad[:, :].rearrange("p (o w) -> p o w", o=1).to_broadcast([P, IDLE, ROW])).then_inc(S["idle_filled"], 16)
            act.wait_ge(S["vecs_in"], 16)
            act.activation(ew[:, 0:1], V("time_decay"), ACT.Exp).then_inc(S["ew_ready"], 1)
            act.wait_ge(S["ew_ready"], 1)
            act.activation(ew[:, 1:2], ew[:, 0:1], ACT.Exp, scale=-1.0).then_inc(S["ew2_ready"], 1)
            act.wait_ge(S["zeroed"], 2)

            def normed_x(c, _):
                after(act, "z1_T", c + 1)
                after(act, "mixed_ready", c)
                act.activation(xn[:, :, 1:L + 1], p_tr[:, :].rearrange("p (b l) -> p b l", b=BPC), ACT.Identity,
                               bias=V("ln1_b"), scale=V("ln1_g")).then_inc(S["xn_ready"], 1)

            def first_apply(c, _):
                after(act, "nm1_ready", c + 1)
                after(act, "z1_T", c)
                after(act, "act_held", c)
                act.activation(held[:, :], V("mix_k"), ACT.Copy).then_inc(S["act_held"], 1)
                for t in range(TPC):
                    xt = x_all[:, bass.ds(c * TPC + t, 1), :].rearrange("p o d -> p (o d)")
                    last = act.activation(z1[:, t, :], xt, ACT.Identity, scale=rs1[:, TPC + t:TPC + t + 1], bias=nm1[:, 1, t:t + 1])
                last.then_inc(S["z1_ready"], 1)

            def first_norm(c, _):
                after(act, "x2_ready", c)
                after(act, "act_held2", c)
                act.activation(held2[:, :], V("mix_k"), ACT.Copy).then_inc(S["act_held2"], 1)
                for t in range(TPC):
                    xt = x_all[:, bass.ds(c * TPC + t, 1), :].rearrange("p o d -> p (o d)")
                    last = act.activation(y1[:, t, :], xt, ACT.Identity, scale=rs1[:, t:t + 1], bias=nm1[:, 0, t:t + 1])
                last.then_inc(S["y1_ready"], 1)

            def second_apply(c, _):
                after(act, "nm2_ready", c + 1)
                after(act, "z2_T", c)
                for t in range(TPC):
                    last = act.activation(z2[:, t, :], x2[:, t, :], ACT.Identity, scale=rs2[:, t:t + 1], bias=nm2[:, t:t + 1])
                last.then_inc(S["z2_ready"], 1)

            def exps(c, _):
                after(act, "k_done", c + 1)
                after(act, "den_ready", c)
                pk = p_k[:, :].rearrange("p (b l) -> p b l", b=BPC)
                act.activation(ek[:, :, 0:1], pk[:, :, 0:1], ACT.Exp, bias=V("time_first"))
                act.activation(ek[:, :, 1:L], pk[:, :, 1:L], ACT.Exp).then_inc(S["exp_done"], 1)
                after(act, "kvr_done", c + 1)
                after(act, "gated_ready", c)
                act.activation(tr[:, :], p_r[:, :], ACT.Tanh, scale=0.5).then_inc(S["gate_r"], 1)

            def normed_y(c, _):
                after(act, "z2_T", c + 1)
                after(act, "ysum_ready", c)
                after(act, "rr_done", c)
                act.activation(yn[:, :, 1:L + 1], p_tr[:, :].rearrange("p (b l) -> p b l", b=BPC), ACT.Identity,
                               bias=V("ln2_b"), scale=V("ln2_g")).then_inc(S["yn_ready"], 1)

            def relus(c, _):
                after(act, "rr_done", c + 1)
                after(act, "ffn_ready", c)
                act.activation(trr[:, :], p_tok[:, :], ACT.Tanh, scale=0.5).then_inc(S["trr_ready"], 1)
                after(act, "kk_ready", FB * c)
                after(act, "fv_done", c)
                for f in range(FB + 1):
                    if f < FB:
                        after(act, "fk_done", FB * c + f + 1)
                        act.activation(hr[:, f, :], p_h[f % 2][:, :], ACT.Relu, scale=0.5).then_inc(S["relu_done"], 1)
                    if f > 0:
                        after(act, "relu_done", FB * c + f)
                        act.activation(kk[:, f - 1, :], hr[:, f - 1, :], ACT.Square).then_inc(S["kk_ready"], 1)

            def normed_m(c, _):
                after(act, "xm_T", c + 1)
                after(act, "scores_done", c)
                act.activation(xmT[:, :], p_tr[:, :], ACT.Copy).then_inc(S["xmT_ready"], 1)

            def copy_rows(c, _):
                after(act, "xm_ready", c + 1)
                after(act, "dispatched", 16 * TPC * TOPK * c)
                act.activation(rows[:, :, :, 0:D], xm[:, :, :].rearrange("p t (o d) -> p t o d", o=1).to_broadcast([P, TPC, TOPK, D]),
                               ACT.Copy).then_inc(S["rows_copied"], 1)

            def gap_exp(c, _):
                after(act, "gap_ready", c + 1)
                after(act, "prob2", c)
                act.activation(egap[:, :], gap[:, :], ACT.Exp).then_inc(S["egap_ready"], 1)

            pipeline(act, [(exps, 0), (normed_m, 2), (first_apply, -1), (gap_exp, 2), (relus, 1), (normed_x, -1), (first_norm, -1),
                           (copy_rows, 2), (second_apply, 0), (normed_y, 0)])

            def turned_rows(s, u):
                after(act, "xg_T", s + 1)
                after(act, "up_done", s - 1)
                act.activation(xgT[u][:, :], p_tr[:, u * P:(u + 1) * P], ACT.Copy).then_inc(S["xgT_ready"], 1)

            def tanh(s, u):
                after(act, "up_done", s + 1)
                after(act, "gate_h_ready", s - 1)
                act.activation(th[u][:, :], p_h[u][:, 0:H], ACT.Tanh, scale=0.5).then_inc(S["tanh_ready"], 1)

            def turned_hidden(s, u):
                after(act, "hid_T", s + 1)
                after(act, "down_done", s - 1)
                act.activation(hidT[u][:, :, :], p_k[:, 0:2 * P].rearrange("p (j m) -> p j m", j=2), ACT.Copy)\
                    .then_inc(S["hidT_ready"], 1)

            pipeline(act, [(tanh, 0), (turned_hidden, 1), (turned_rows, -1)], SLOTS, 2, 4)
            for c in range(CHUNKS):
                act.wait_ge(S["o_add2"], c + 1)
                act.dma_start(out[:, c * TPC:(c + 1) * TPC, :], x_all[:, c * TPC:(c + 1) * TPC, :]).then_inc(S["stored"], 16)
            act.wait_ge(S["stored"], 16 * CHUNKS)

        @block.tensor
        def _(pe):
            pe.wait_ge(S["ident_ready"], 1)
            pe.wait_ge(S["weights_in"], 16)
            pe.wait_ge(S["consts"], 8)

            def turn_tiles(src, done):
                for t in range(TPC):
                    mm = pe.transpose(p_tr[:, t * P:(t + 1) * P], src[:, t, :], ident[:, :])
                mm.then_inc(S[done], 1)

            def turn_x(c, _):
                after(pe, "z1_ready", c + 1)
                after(pe, "xmT_ready", c - 2)
                after(pe, "yn_ready", c - 1)
                turn_tiles(z1, "z1_T")

            def kvr(c, _):
                after(pe, "mixed_ready", c + 1)
                after(pe, "exp_done", c)
                pe.matmul(p_k[:, :], W("Wk"), mixed[0][:, :, :].rearrange("p b l -> p (b l)"), start=True, stop=True)\
                    .then_inc(S["k_done"], 1)
                after(pe, "ekv_ready", c)
                pe.matmul(p_v[:, :], W("Wv"), mixed[1][:, :, :].rearrange("p b l -> p (b l)"), start=True, stop=True)\
                    .then_inc(S["v_done"], 1)
                after(pe, "gate_r", c)
                after(pe, "spot_ready", c - 2)
                pe.matmul(p_r[:, :], W("Wr"), mixed[2][:, :, :].rearrange("p b l -> p (b l)"), start=True, stop=True)\
                    .then_inc(S["kvr_done"], 1)

            def attn_out(c, _):
                after(pe, "rw_ready", c + 1)
                after(pe, "trr_ready", c)
                for t in range(TPC):
                    mm = pe.matmul(p_tok[:, t * P:(t + 1) * P], rw[:, t * P:(t + 1) * P], W("Wo"),
                                   start=True, stop=True)
                mm.then_inc(S["wo_done"], 1)

            def turn_y(c, _):
                after(pe, "z2_ready", c + 1)
                after(pe, "xn_ready", c + 2 if not isinstance(c, int) else min(c + 2, CHUNKS))
                turn_tiles(z2, "z2_T")

            def ffn_in(c, _):
                after(pe, "yn_ready", c + 1)
                after(pe, "x2_ready", c + 1)
                for t in range(TPC):
                    tile = yn[:, t // 2, 1 + (t % 2) * P:1 + (t % 2 + 1) * P]
                    mm = pe.matmul(p_tok[:, t * P:(t + 1) * P], tile, W("Wfr"), start=True, stop=True)
                mm.then_inc(S["rr_done"], 1)
                after(pe, "ysum_ready", c + 1)
                for f in range(FB):
                    after(pe, "relu_done", FB * c + f - 1)
                    pe.matmul(p_h[f % 2][:, :], W("Wfk")[:, f * P:(f + 1) * P],
                              ysum[:, :, :].rearrange("p b l -> p (b l)"), start=True, stop=True)\
                        .then_inc(S["fk_done"], 1)

            def ffn_out(c, _):
                after(pe, "kk_ready", FB * (c + 1))
                after(pe, "ffn_ready", c)
                for t in range(TPC):
                    for f in range(FB):
                        mm = pe.matmul(p_f[:, t * P:(t + 1) * P], kk[:, f, t * P:(t + 1) * P],
                                       W("Wfv")[:, f * P:(f + 1) * P], start=(f == 0), stop=(f == FB - 1))
                mm.then_inc(S["fv_done"], 1)

            def turn_m(c, _):
                after(pe, "xm_ready", c + 1)
                after(pe, "yn_ready", c + 2 if not isinstance(c, int) else min(c + 2, CHUNKS))
                turn_tiles(xm, "xm_T")

            def scores(c, _):
                after(pe, "xmT_ready", c + 1)
                after(pe, "gate_r", c + 3 if not isinstance(c, int) else min(c + 3, CHUNKS))
                for t in range(TPC):
                    mm = pe.matmul(p_r[:, t * E:(t + 1) * E], xmT[:, t * P:(t + 1) * P], W("gate"), start=True, stop=True)
                mm.then_inc(S["scores_done"], 1)

            def ranks(c, _):
                after(pe, "both_ready", c + 1)
                after(pe, "scores_in", c + 1)
                r = p_r[:, 0:TPC * E].rearrange("p (t e) -> p t e", t=TPC)
                after(pe, "seen_ready", c + 1)
                pe.matmul(r, tri[:, :], both[:, :, :], start=True, stop=False)
                for t in range(TPC - 1):
                    pe.matmul(r[:, t + 1:, :], ones[:, :], both[:, t:t + 1, :].to_broadcast([P, TPC - 1 - t, E]),
                              start=False, stop=False)
                pe.matmul(r, ones[:, :], seen[:, :].rearrange("p (o e) -> p o e", o=1).to_broadcast([P, TPC, E]),
                          start=False, stop=True).then_inc(S["rank_done"], 1)

            pipeline(pe, [(kvr, 0), (turn_m, 2), (scores, 2), (ffn_in, 1), (turn_x, -1), (ranks, 2), (ffn_out, 1), (attn_out, 0), (turn_y, 0)])

            pe.wait_ge(S["seen_ready"], CHUNKS + 1)
            pe.wait_ge(S["spot_ready"], CHUNKS)
            pe.matmul(p_r[:, 0:E], ones[:, :], seen[:, :], start=True, stop=True).then_inc(S["total_done"], 1)

            pe.wait_ge(S["table_w"], 1)
            pe.wait_ge(S["w12_in"], 16)
            pe.wait_ge(S["w3_in"], 16)

            def turn_rows(s, u):
                after_loaded(pe, s, u)
                after(pe, "xgT_ready", s - 1)
                pe.transpose(p_tr[:, (u % 2) * P:(u % 2 + 1) * P], xg[u][:, 0:D], ident[:, :]).then_inc(S["xg_T"], 1)

            def up(s, u):
                w = pe.value_load(slot_w[0:1, bass.ds(s, 1)], min_val=0, max_val=E - 1)
                after(pe, "xgT_ready", s + 1)
                after(pe, "hid_ready", s - 1)
                pe.matmul(p_h[u % 2][:, :], xgT[u % 2][:, :], w12_sb[:, bass.ds(w * (2 * H), 2 * H)], start=True, stop=True)\
                    .then_inc(S["up_done"], 1)

            def turn_hidden(s, u):
                after(pe, "hid_ready", s + 1)
                after(pe, "hidT_ready", s)
                for j in range(2):
                    mm = pe.transpose(p_k[:, j * P:(j + 1) * P], hid[u % 2][:, j * P:(j + 1) * P], ident[:, :])
                mm.then_inc(S["hid_T"], 1)

            def down(s, u):
                w = pe.value_load(slot_w[0:1, bass.ds(s, 1)], min_val=0, max_val=E - 1)
                after(pe, "hidT_ready", s + 1)
                after(pe, "yo_ready", s - 1)
                p_y = (p_v, p_r)[u % 2]
                for j in range(2):
                    mm = pe.matmul(p_y[:, 0:D], hidT[u % 2][:, j, :], w3_sb[:, bass.ds(w * (2 * D) + j * D, D)],
                                   start=(j == 0), stop=(j == 1))
                mm.then_inc(S["down_done"], 1)

            pipeline(pe, [(up, 0), (down, 2), (turn_hidden, 1), (turn_rows, -1)], SLOTS, BUFS, BUFS)

        @block.vector
        def _(dve):
            dve.wait_ge(S["ew2_ready"], 1)
            dve.memset(decay[:, :], 0.0).then_inc(S["decay_ready"], 1)
            dve.wait_ge(S["decay_ready"], 1)
            dv = decay[:, :].rearrange("p (b l) -> p b l", b=BPC)
            dve.tensor_scalar(dv[:, :, 1:L], dv[:, :, 1:L], ew[:, 1:2], None, ALU.add).then_inc(S["decay_ready"], 1)
            dve.wait_ge(S["decay_ready"], 2)
            dve.memset(seen[:, :], 0.0).then_inc(S["seen_ready"], 1)
            dve.wait_ge(S["consts"], 8)

            def moments(src, st, mv, dm, which, c):
                for t in range(TPC):
                    last = dve.bn_stats(st[:, t, :], src(t))
                last.then_inc(S[which + "_stats"], 1)
                after(dve, which + "_stats", c + 1)
                dve.tensor_tensor(dm[:, :], st[:, :, 1], st[:, :, 4], ALU.subtract).then_inc(S[which + "_halves"], 1)
                dve.tensor_tensor(mv[:, :, :], st[:, :, 1:3], st[:, :, 4:6], ALU.add).then_inc(S[which + "_sums"], 1)
                after(dve, which + "_halves", c + 1)
                dve.tensor_tensor(dm[:, :], dm[:, :], dm[:, :], ALU.mult).then_inc(S[which + "_sq"], 1)
                after(dve, which + "_sums", c + 1)
                dve.tensor_scalar(mv[:, :, 0], mv[:, :, 0], -0.5, None, ALU.mult).then_inc(S[which + "_mean"], 1)
                after(dve, which + "_sq", c + 1)
                dve.scalar_tensor_tensor(out=mv[:, :, 1], in0=dm[:, :], scalar=D / 4, in1=mv[:, :, 1],
                                         op0=ALU.mult, op1=ALU.add).then_inc(S[which + "_moments"], 1)
                after(dve, which + "_moments", c + 1)

            def ln1(c, _):
                if isinstance(c, int) and c < 2:
                    dve.wait_ge(S["x_first" if c == 0 else "x_second"], 16)
                else:
                    dve.wait_ge(S["x_rest"], 16)
                moments(lambda t: x_all[:, bass.ds(c * TPC + t, 1), :].rearrange("p o d -> p (o d)"), st1, mv1, dm1, "ln1", c)
                v = mv1[:, :, 1]
                dve.tensor_scalar(var1[:, 0:TPC], v, 1.0 / D, LN_EPS, ALU.mult, ALU.add)
                dve.tensor_scalar(var1[:, TPC:], v, (1.0 + LN_EPS) / D, LN_EPS * LN_EPS, ALU.mult, ALU.add)\
                    .then_inc(S["ln1_var"], 1)

            def mixes(c, _):
                after(dve, "dif_ready", c + 1)
                after(dve, "kvr_done", c)
                for n, m in enumerate(["mix_k", "mix_v", "mix_r"]):
                    last = dve.scalar_tensor_tensor(out=mixed[n][:, :, :], in0=dif[:, :, :], scalar=V(m),
                                                    in1=xn[:, :, 0:L], op0=ALU.mult, op1=ALU.add)
                last.then_inc(S["mixed_ready"], 1)

            def wkv(c, _):
                after(dve, "exp_done", c + 1)
                after(dve, "v_done", c + 1)
                ekf = ek[:, :, :].rearrange("p b l -> p (b l)")
                dve.tensor_tensor(ekv[:, :], ekf, p_v[:, :], ALU.mult).then_inc(S["ekv_ready"], 1)
                dve.tensor_tensor_scan(den[:, :], decay[:, :], ekf, 0.0, ALU.mult, ALU.add).then_inc(S["den_ready"], 1)
                after(dve, "den_ready", c + 1)
                dve.tensor_scalar(den[:, :], den[:, :], WKV_EPS, None, ALU.add).then_inc(S["den_eps"], 1)
                after(dve, "ekv_ready", c + 1)
                dve.tensor_tensor_scan(num[:, :], decay[:, :], ekv[:, :], 0.0, ALU.mult, ALU.add)\
                    .then_inc(S["num_ready"], 1)
                after(dve, "den_eps", c + 1)
                dve.reciprocal(rden[:, :], den[:, :]).then_inc(S["rden_ready"], 1)
                after(dve, "gate_r", c + 1)
                after(dve, "num_ready", c + 1)
                dve.scalar_tensor_tensor(out=gated[:, :], in0=tr[:, :], scalar=1.0, in1=num[:, :],
                                         op0=ALU.add, op1=ALU.mult).then_inc(S["gated_ready"], 1)
                after(dve, "gated_ready", c + 1)
                after(dve, "rden_ready", c + 1)
                after(dve, "wo_done", c)
                dve.tensor_tensor(rw[:, :], gated[:, :], rden[:, :], ALU.mult).then_inc(S["rw_ready"], 1)

            def ln2(c, _):
                after(dve, "wo_done", c + 1)
                after(dve, "y1_ready", c + 1)
                after(dve, "res_ready", c)
                dve.scalar_tensor_tensor(out=x2[:, :, :], in0=p_tok[:, :].rearrange("p (t d) -> p t d", t=TPC),
                                         scalar=0.5, in1=y1[:, :, :], op0=ALU.mult, op1=ALU.add)\
                    .then_inc(S["x2_ready"], 1)
                after(dve, "x2_ready", c + 1)
                moments(lambda t: x2[:, t, :], st2, mv2, dm2, "ln2", c)
                dve.tensor_scalar(var2[:, :], mv2[:, :, 1], 1.0 / D, LN_EPS, ALU.mult, ALU.add).then_inc(S["ln2_var"], 1)

            def ln3(c, _):
                after(dve, "fv_done", c + 1)
                after(dve, "trr_ready", c + 1)
                dve.scalar_tensor_tensor(out=ffn[:, :], in0=trr[:, :], scalar=1.0, in1=p_f[:, :],
                                         op0=ALU.add, op1=ALU.mult).then_inc(S["ffn_ready"], 1)
                after(dve, "ffn_ready", c + 1)
                after(dve, "res_ready", c + 1)
                after(dve, "x3_kept", 16 * c)
                dve.scalar_tensor_tensor(out=x3[:, :, :], in0=ffn[:, :].rearrange("p (t d) -> p t d", t=TPC),
                                         scalar=0.5, in1=x_all[:, tiles_of(c), :], op0=ALU.mult, op1=ALU.add)\
                    .then_inc(S["x3_ready"], 1)
                after(dve, "x3_ready", c + 1)
                moments(lambda t: x3[:, t, :], st3, mv3, dm3, "ln3", c)
                dve.tensor_scalar(var3[:, :], mv3[:, :, 1], 1.0 / D, LN_EPS, ALU.mult, ALU.add).then_inc(S["ln3_var"], 1)

            def ln3_apply(c, _):
                after(dve, "ln3_rstd", c + 1)
                after(dve, "xm_T", c)
                after(dve, "rows_copied", c)
                for t in range(TPC):
                    last = dve.tensor_scalar(xm[:, t, :], x3[:, t, :], mv3[:, t, 0:1], rs3[:, t:t + 1],
                                             ALU.add, ALU.mult)
                last.then_inc(S["xm_ready"], 1)

            def flat(ap, o):
                return ap.rearrange("p (t o) -> p t o", o=1).to_broadcast([P, TPC, E])

            PICKS = 11

            def picked(c, ins, n):
                ins.then_inc(S["picking"], 1)
                after(dve, "picking", c * PICKS + n)

            def pick_one(c, k, n):
                picked(c, dve.tensor_reduce(best[:, k, :], sc[:, :, :], mybir.AxisListType.X, ALU.max), n + 1)
                picked(c, dve.tensor_tensor(eq[:, :, :], sc[:, :, :], flat(best[:, k, :], E), ALU.is_equal), n + 2)
                picked(c, dve.tensor_tensor(eq[:, :, :], eq[:, :, :], rev[:, :, :], ALU.mult), n + 3)
                picked(c, dve.tensor_reduce(low[:, :], eq[:, :, :], mybir.AxisListType.X, ALU.max), n + 4)
                picked(c, dve.tensor_tensor(hot[:, k, :, :], rev[:, :, :], flat(low[:, :], E), ALU.is_equal), n + 5)

            def pick(c, _):
                after(dve, "scores_done", c + 1)
                dve.tensor_copy(sc[:, :, :], p_r[:, 0:TPC * E].rearrange("p (t e) -> p t e", t=TPC)).then_inc(S["scores_in"], 1)
                after(dve, "scores_in", c + 1)
                pick_one(c, 0, 0)
                picked(c, dve.scalar_tensor_tensor(out=sc[:, :, :], in0=hot[:, 0, :, :], scalar=-3.0e38, in1=sc[:, :, :],
                                                   op0=ALU.mult, op1=ALU.add), 6)
                pick_one(c, 1, 6)
                after(dve, "rank_done", c)
                dve.tensor_tensor(both[:, :, :], hot[:, 0, :, :], hot[:, 1, :, :], ALU.add).then_inc(S["both_ready"], 1)
                dve.tensor_tensor(gap[:, :], best[:, 1, :], best[:, 0, :], ALU.subtract).then_inc(S["gap_ready"], 1)

            def place(c, _):
                after(dve, "egap_ready", c + 1)
                dve.tensor_scalar(esum[:, :], egap[:, :], 1.0, None, ALU.add).then_inc(S["esum_ready"], 1)
                after(dve, "dispatched", 16 * TPC * TOPK * c)
                dve.tensor_copy(rows[:, :, :, D:D + 1].bitcast(I32),
                                ids[:, tiles_of(c), :].rearrange("p t (k o) -> p t k o", o=1)).then_inc(S["ids_in"], 1)
                after(dve, "esum_ready", c + 1)
                dve.reciprocal(prob[:, :, 0], esum[:, :]).then_inc(S["prob1"], 1)
                after(dve, "prob1", c + 1)
                dve.tensor_copy(rows[:, :, 0, D + 1], prob[:, :, 0])
                dve.tensor_tensor(rows[:, :, 1, D + 1], prob[:, :, 0], egap[:, :], ALU.mult).then_inc(S["prob2"], 1)
                after(dve, "rank_done", c + 1)
                dve.tensor_tensor(spot[:, :, :], region[:, :, :], p_r[:, 0:TPC * E].rearrange("p (t e) -> p t e", t=TPC),
                                  ALU.add).then_inc(S["spot_ready"], 1)
                dve.tensor_reduce(chunk_seen[:, :], both[:, :, :].rearrange("p t e -> p e t"), mybir.AxisListType.X,
                                  ALU.add).then_inc(S["chunk_seen_ready"], 1)
                after(dve, "spot_ready", c + 1)
                for k in range(TOPK):
                    last = dve.tensor_tensor(spots[:, k, :, :], hot[:, k, :, :], spot[:, :, :], ALU.mult)
                last.then_inc(S["spots_ready"], 1)
                after(dve, "chunk_seen_ready", c + 1)
                dve.tensor_tensor(seen[:, :], seen[:, :], chunk_seen[:, :], ALU.add).then_inc(S["seen_ready"], 1)
                after(dve, "spots_ready", c + 1)
                with nc.allow_low_precision(reason="whole numbers under 2**24, summed in float32"):
                    dve.tensor_reduce(pos[:, :, :], spots[:, :, :, :], mybir.AxisListType.X, ALU.add)\
                        .then_inc(S["pos_ready"], 1)

            pipeline(dve, [(ln1, -1), (pick, 2), (wkv, 0), (place, 2), (ln3, 1), (ln2, 0), (ln3_apply, 1), (mixes, -1)])

            steps_made = [0]

            def link(ins):
                steps_made[0] += 1
                ins.then_inc(S["table_steps"], 1)
                dve.wait_ge(S["table_steps"], steps_made[0])

            dve.wait_ge(S["total_done"], 1)
            link(dve.tensor_copy(total[:, :], p_r[:, 0:E]))
            dve.tensor_copy(total_i[:, :], total[:, :]).then_inc(S["total_int"], 1)
            link(dve.tensor_scalar(ntile_i[:, :], total[:, :], float(P - 1), None, ALU.add))
            link(dve.tensor_scalar(ntile_i[:, :], ntile_i[:, :], P.bit_length() - 1, None, ALU.arith_shift_right))
            link(dve.tensor_copy(ntile[:, :], ntile_i[:, :]))
            link(dve.tensor_tensor_scan(cum[:, :], ones_e[:, :], ntile[:, :], 0.0, ALU.mult, ALU.add))
            over_e = lambda ap: ap.rearrange("p (s o) -> p s o", o=1).to_broadcast([P, SLOTS, E])
            over_s = lambda ap: ap.rearrange("p (o e) -> p o e", o=1).to_broadcast([P, SLOTS, E])
            link(dve.tensor_tensor(past[:, :, :], over_e(slot_no[:, :]), over_s(cum[:, :]), ALU.is_ge))
            link(dve.tensor_reduce(slot_e[:, :], past[:, :, :], mybir.AxisListType.X, ALU.add))
            dve.tensor_scalar(slot_w[:, :], slot_e[:, :], float(E - 1), None, ALU.min).then_inc(S["table_w"], 1)
            link(dve.tensor_tensor(past_tiles[:, :, :], past[:, :, :], over_s(ntile[:, :]), ALU.mult))
            link(dve.tensor_reduce(slot_first[:, :], past_tiles[:, :, :], mybir.AxisListType.X, ALU.add))
            link(dve.tensor_tensor(slot_first[:, :], slot_no[:, :], slot_first[:, :], ALU.subtract))
            link(dve.tensor_scalar(slot_first[:, :], slot_first[:, :], float(P), None, ALU.mult))
            dve.scalar_tensor_tensor(out=slot_row[:, :], in0=slot_e[:, :], scalar=float(REGION), in1=slot_first[:, :],
                                     op0=ALU.mult, op1=ALU.add).then_inc(S["table_row"], 1)

            def gate_hidden(s, u):
                after(dve, "tanh_ready", s + 1)
                after(dve, "hid_ready", s)
                dve.scalar_tensor_tensor(out=gate_h[:, :], in0=th[u % 2][:, :], scalar=1.0, in1=p_h[u % 2][:, 0:H],
                                         op0=ALU.add, op1=ALU.mult).then_inc(S["gate_h_ready"], 1)
                after(dve, "gate_h_ready", s + 1)
                after(dve, "hid_T", s - 1)
                dve.tensor_tensor(hid[u % 2][:, :], gate_h[:, :], p_h[u % 2][:, H:2 * H], ALU.mult).then_inc(S["hid_ready"], 1)

            def weigh(s, u):
                after(dve, "down_done", s + 1)
                after(dve, f"scattered{u}", 16 // BUFS * (s - u))
                p_y = (p_v, p_r)[u % 2]
                dve.tensor_scalar(yo[u][:, :], p_y[:, 0:D], xg[u][:, D + 1:D + 2], 0.5, ALU.mult, ALU.mult)\
                    .then_inc(S["yo_ready"], 1)

            pipeline(dve, [(gate_hidden, 0), (weigh, 2)], SLOTS, BUFS, BUFS)

            for c in range(CHUNKS):
                dve.wait_ge(S[f"o_in{c}"], 16)
                dve.wait_ge(S["x3_kept"], 16 * CHUNKS)
                part = slice(c * TPC, (c + 1) * TPC)
                dve.tensor_tensor(x_all[:, part, :], x_all[:, part, :], o_all[:, part, 0, :], ALU.add).then_inc(S["o_add1"], 1)
                dve.wait_ge(S["o_add1"], c + 1)
                dve.tensor_tensor(x_all[:, part, :], x_all[:, part, :], o_all[:, part, 1, :], ALU.add).then_inc(S["o_add2"], 1)


def kernel(**inputs):
    import numpy as np
    import concourse.bacc as bacc
    from concourse.bass_utils import run_bass_kernel_spmd as run

    a = {k.replace("L0_attn_", "").replace("L0_ffn_", ""): np.asarray(v) for k, v in inputs.items()}
    arrays = {
        "x": a["x"].reshape(TILES, P, D).transpose(1, 0, 2),
        "weights": np.concatenate([a["Wk"], a["Wv"], a["Wr"], a["Wo"], a["Wfr"], a["Wfk"],
                                   a["Wfv"].reshape(FB, P, D).transpose(1, 0, 2).reshape(P, FFN),
                                   a["gate_w"].T], axis=1),
        "vecs": np.stack([a[n] for n in VEC], axis=1),
        "w12": a["w12"].transpose(2, 0, 1).reshape(P, E * 2 * H),
        "w3": a["w3"].transpose(2, 0, 1).reshape(2, P, E, D).transpose(1, 2, 0, 3).reshape(P, E * 2 * D),
    }
    arrays = {k: np.ascontiguousarray(v) for k, v in arrays.items()}
    nc = bacc.Bacc("TRN2", target_bir_lowering=False, num_devices=1)
    args = [nc.dram_tensor(k, v.shape, F32, kind="ExternalInput").ap() for k, v in arrays.items()]
    args.append(nc.dram_tensor("out", [P, TILES, D], F32, kind="ExternalOutput").ap())
    build(nc, *args)
    r = run(nc, [arrays], core_ids=[0])
    return r.results[0]["out"].transpose(1, 0, 2).reshape(B, L, D)
```

```python
import concourse.bass as bass
from concourse import mybir
from concourse.alu_op_type import AluOpType as ALU
from contextlib import ExitStack

F32 = mybir.dt.float32
BF16 = mybir.dt.bfloat16
I32 = mybir.dt.int32
U32 = mybir.dt.uint32
ACT = mybir.ActivationFunctionType

B, L, D = 16, 256, 128
P = 128
TOKENS = B * L
TILES = TOKENS // P
TPC = 4
CT = TPC * P
BPC = CT // L
CHUNKS = TILES // TPC
FFN = 4 * D
FB = FFN // P
E, H = 8, 256
LN_EPS = 1e-5
WKV_EPS = 1e-8
VEC = {n: i for i, n in enumerate(
    ["ln1_g", "ln1_b", "mix_k", "mix_v", "mix_r", "ln2_g", "ln2_b", "time_decay", "time_first"])}
WOFF = {}
_at = 0
for _n, _w in [("Wk", D), ("Wv", D), ("Wr", D), ("Wo", D), ("Wfr", D), ("Wfk", FFN), ("Wfv", FFN), ("gate", E)]:
    WOFF[_n] = (_at, _at + _w)
    _at += _w
WCOLS = _at
TOPK = 2
ROW = D + 2
REGION = TOKENS + P
EW = 2 * H + 2 * D
SLOTS = TOKENS * TOPK // P + E
IDLE = E
RESULTS = TOKENS * TOPK
PAIRS = SLOTS // 2
BUFS = 6
EARLY = 3
NOWHERE = 2 * RESULTS


def build(nc, x_in, w_in, v_in, experts_in, out):
    ctx = ExitStack()
    with ctx:
        def sb(name, shape, dt=F32):
            return ctx.enter_context(nc.sbuf_tensor(name, shape, dt))

        def bank(name):
            return ctx.enter_context(nc.psum_tensor(name, [P, CT], F32))

        def sem(name):
            return ctx.enter_context(nc.semaphore(name))

        x_all = sb("x_all", [P, TILES, D])
        w_sb = sb("w_sb", [P, WCOLS])
        vec = sb("vec", [P, len(VEC)])
        ident = sb("ident", [P, P])
        decay = sb("decay", [P, CT])
        ew = sb("ew", [P, 2])
        neg_half = sb("neg_half", [P, 2, TILES])

        st1 = sb("st1", [P, TPC, 6]); mv1 = sb("mv1", [P, TPC, 2]); neg1 = sb("neg1", [P, TILES])
        st2 = sb("st2", [P, TPC, 6]); mv2 = sb("mv2", [P, TPC, 2]); neg2 = sb("neg2", [P, TPC])
        st3 = sb("st3", [P, TPC, 6]); mv3 = sb("mv3", [P, TPC, 2])
        var1 = sb("var1", [P, 2, TILES]); rs1 = sb("rs1", [P, 2, TILES])
        var2 = sb("var2", [P, TPC]); rs2 = sb("rs2", [P, TPC])
        var3 = sb("var3", [P, TPC]); rs3 = sb("rs3", [P, TPC])
        nm1 = sb("nm1", [P, 2, TILES]); nm2 = sb("nm2", [P, TPC])
        z1_wait = sb("z1_wait", [P, 1]); y1_wait = sb("y1_wait", [P, 1]); late_mark = sb("late_mark", [P, 1])
        moments_wait = sb("moments_wait", [P, 3])
        z1 = sb("z1", [P, TPC, D]); y1 = sb("y1", [P, TPC, D])
        xn = sb("xn", [P, BPC, L + 1])
        rest_mix = sb("rest_mix", [P, 3]); w_mix = sb("w_mix", [P, 3, 2, D]); wfv_half = sb("wfv_half", [P, FFN])
        ek = sb("ek", [P, BPC, L]); ekv = sb("ekv", [P, CT])
        tr = sb("tr", [P, CT]); num = sb("num", [P, CT]); den = sb("den", [P, CT])
        rden = sb("rden", [P, CT]); gated = sb("gated", [P, CT]); rw = sb("rw", [P, CT])
        x2 = sb("x2", [P, TPC, D]); z2 = sb("z2", [P, TPC, D])
        yn = sb("yn", [P, BPC, L + 1]); ysum = sb("ysum", [P, BPC, L])
        trr = sb("trr", [P, CT]); hr = sb("hr", [P, FB, CT]); kk = sb("kk", [P, FB, CT])
        ffn = sb("ffn", [P, CT]); x3 = sb("x3", [P, TPC, D]); xm = sb("xm", [P, TPC, D]); xmT = sb("xmT", [P, CT])

        rows_of = [sb(f"rows{n}", [P, TPC, TOPK, ROW]) for n in range(2)]
        pad = sb("pad", [P, ROW])
        tri = sb("tri", [P, P], BF16); ones = sb("ones", [P, P], BF16)
        rev = sb("rev", [P, TPC, E]); region = sb("region", [P, TPC, E]); token_no = sb("token_no", [P, TILES])
        sc = sb("sc", [P, TPC, E]); eq = sb("eq", [P, TPC, E])
        low = sb("low", [P, TOPK, TPC]); higher = sb("higher", [P, TOPK, TPC])
        best = sb("best", [P, TOPK, TPC]); hot = sb("hot", [P, TOPK, TPC, E]); both = sb("both", [P, TPC, E], BF16)
        gap = sb("gap", [P, TPC]); egap = sb("egap", [P, TPC])
        esum = sb("esum", [P, TPC]); prob = sb("prob", [P, TPC, TOPK])
        seen = sb("seen", [P, E], BF16); chunk_seen = sb("chunk_seen", [P, E], BF16)
        spot = sb("spot", [P, TPC, E]); spots = sb("spots", [P, TOPK, TPC, E])
        pos_of = [sb(f"pos{n}", [P, TOPK, TPC], U32) for n in range(2)]
        total = sb("total", [P, E]); total_i = sb("total_i", [P, E], I32)
        ntile_i = sb("ntile_i", [P, E], I32); ntile = sb("ntile", [P, E]); cum = sb("cum", [P, E])
        ones_e = sb("ones_e", [P, E]); slot_no = sb("slot_no", [P, SLOTS])
        past = sb("past", [P, SLOTS, E]); past_tiles = sb("past_tiles", [P, SLOTS, E])
        slot_e = sb("slot_e", [P, SLOTS]); slot_first = sb("slot_first", [P, SLOTS])
        slot_row = sb("slot_row", [P, SLOTS], I32); slot_w = sb("slot_w", [P, SLOTS], I32)
        pair_slot = sb("pair_slot", [P, BUFS, PAIRS // BUFS]); used = sb("used", [P, TOPK, BUFS, PAIRS // BUFS])
        pair_end = sb("pair_end", [P, EARLY]); is_late = sb("is_late", [P, EARLY])
        late_wait = sb("late_wait", [P, EARLY], I32)
        rounds_used = sb("rounds_used", [P, TOPK, BUFS]); last_scatter = sb("last_scatter", [P, TOPK, BUFS], I32)
        w_exp = sb("w_exp", [P, E * EW])
        xg = [sb(f"xg{n}", [P, 2, ROW]) for n in range(BUFS)]
        xgT = [sb(f"xgT{n}", [P, 2, P]) for n in range(2)]
        w_up = [sb(f"w_up{n}", [P, 2, 2 * H]) for n in range(2)]
        th = sb("th", [P, 2, H]); gate_h = sb("gate_h", [P, 2, H])
        hid = [sb(f"hid{n}", [P, 2, H // P, P]) for n in range(2)]
        yo = [sb(f"yo{n}", [P, 2, D]) for n in range(BUFS)]
        result_row = [sb(f"result_row{n}", [P, 2], U32) for n in range(BUFS)]
        o_all = sb("o_all", [P, TOPK, TILES, D])

        rows_d = nc.dram_tensor("rows_d", [E * REGION + IDLE * P, ROW], F32, kind="Internal").ap()
        res_d = nc.dram_tensor("res_d", [RESULTS, D], F32, kind="Internal").ap()

        p_up = [ctx.enter_context(nc.psum_tensor(f"p_up{n}", [P, 2, CT], F32)) for n in range(2)]
        p_h = [p_up[0][:, 0, :], p_up[0][:, 1, :]]; p_k = p_up[1][:, 0, :]; p_v = p_up[1][:, 1, :]
        p_tr = bank("p_tr"); p_r = bank("p_r"); p_tok = bank("p_tok"); p_f = bank("p_f")

        names = """x_first x_second x_rest weights_in vecs_in zeroed ident_ready halves ew_ready ew2_ready decay_ready
        ln1_stats ln1_moments ln1_var ln1_rstd z1_ready nm1_ready nm2_ready y1_ready z1_T xn_ready
        r_done k_done v_done exp_done gate_r gate_r1 ekv_ready num_ready den_ready den_eps rden_ready gated_ready rw_ready
        wo_done x2_ready res_ready ln2_stats ln2_moments ln2_var ln2_rstd z2_ready z2_T yn_ready ysum_ready
        rr_done trr_ready fk_done relu_done kk_ready fv_done ffn_ready x3_ready mix_rest_ready w_mixed
        ln3_stats x3_kept ln3_moments ln3_var ln3_rstd xm_ready xm_T xmT_ready scores_done stored
        pads consts scores_in picking both_ready gap_ready egap_ready
        esum_ready prob1 prob2 chunk_seen_ready seen_ready rank_done spot_ready spots_ready pos_ready rows_copied
        labelled order_known
        dispatched idle_filled pad_filled last_dispatched late_rows late_wait_ready
        total_done total_int table_steps table_w table_row table_used
        z1_wait_taken y1_wait_taken experts_in
        xg_T xgT_ready up_done tanh_ready gate_h_ready hid_ready down_done
        yo_ready""".split() + [f"o_in{k}_{c}" for k in range(TOPK) for c in range(CHUNKS)]\
            + ["lower_added", "lower_added_pool", "higher_added"]
        names += [f"{n}{b}" for n in ("xg_loaded", "scattered") for b in range(BUFS)]
        S = {n: sem(n) for n in names}

        def W(n):
            a, b = WOFF[n]
            return w_sb[:, a:b]

        def V(n):
            return vec[:, VEC[n]:VEC[n] + 1]

        def is_last(c):
            return isinstance(c, int) and c == CHUNKS - 1

        def after_dispatched(eng, c):
            if not is_last(c):
                after(eng, "dispatched", 16 * TPC * TOPK * c)

        def after(eng, name, count):
            if isinstance(count, int) and count <= 0:
                return
            eng.wait_ge(S[name], count)

        def upto(count):
            return min(count, CHUNKS) if isinstance(count, int) else count

        LN1_GROUPS = [(0, 1), (1, 2), (2, 5), (5, CHUNKS)]

        def after_ln1(eng, c):
            group = [n for n, (first, last) in enumerate(LN1_GROUPS) if not isinstance(c, int) or first <= c < last][-1]
            eng.wait_ge(S["nm1_ready"], group + 1)

        def tiles(c):
            return slice(c * TPC, (c + 1) * TPC)

        def tiles_of(c):
            return bass.ds(c * TPC, TPC)

        block = ctx.enter_context(nc.Block())

        def pipeline(eng, steps):
            lags = [lag for _, lag in steps]
            first, last = min(lags), CHUNKS - 1 + max(lags)
            lo, hi = max(lags) + 1, CHUNKS - 1 + min(lags)

            def turn(i):
                for step, lag in steps:
                    if not isinstance(i, int) or 0 <= i - lag < CHUNKS:
                        step(i - lag)

            for i in range(first, lo):
                turn(i)
            with eng.Fori(lo, hi + 1) as i:
                turn(i)
            for i in range(hi + 1, last + 1):
                turn(i)

        def rounds(eng, steps, first_round):
            lags = [lag for _, lag in steps]
            last_round = (PAIRS - 1 + min(lags) - (BUFS - 1)) // BUFS

            def turn(r, u):
                for step, lag in steps:
                    if not isinstance(r, int) or 0 <= r * BUFS + u - lag < PAIRS:
                        off, place = divmod(u - lag, BUFS)
                        step(r * BUFS + (u - lag), r + off, place)

            for i in range(min(lags), first_round * BUFS):
                turn(i // BUFS, i % BUFS)
            with eng.Fori(first_round, last_round + 1) as r:
                for u in range(BUFS):
                    turn(r, u)
            for i in range((last_round + 1) * BUFS, PAIRS + max(lags)):
                turn(i // BUFS, i % BUFS)

        def fill_pads(eng, experts):
            for e in experts:
                n = eng.value_load(total_i[0:1, e:e + 1], min_val=0, max_val=TOKENS)
                eng.dma_start(rows_d[bass.ds(n + e * REGION, P), :], pad[:, :]).then_inc(S["pad_filled"], 16)

        DVE_CHUNKS = 5

        def add_result(eng, k, c, done):
            eng.wait_ge(S[f"o_in{k}_{c}"], 16)
            eng.tensor_tensor(x_all[:, tiles(c), :], x_all[:, tiles(c), :], o_all[:, k, tiles(c), :],
                              ALU.add).then_inc(S[done], 1)

        @block.sync
        def _(sp):
            sp.dma_start(x_all[:, 0:TPC, :], x_in[:, 0:TPC, :]).then_inc(S["x_first"], 16)
            sp.dma_start(x_all[:, TPC:2 * TPC, :], x_in[:, TPC:2 * TPC, :]).then_inc(S["x_second"], 16)
            sp.dma_start(x_all[:, 2 * TPC:, :], x_in[:, 2 * TPC:, :]).then_inc(S["x_rest"], 16)

            def keep(c):
                after(sp, "x3_ready", c + 1)
                sp.dma_start(x_all[:, tiles_of(c), :], x3[:, :, :]).then_inc(S["x3_kept"], 16)

            pipeline(sp, [(keep, 0)])

            sp.wait_ge(S["total_int"], 1)
            sp.wait_ge(S["pads"], 3)
            fill_pads(sp, range(0, E, 2))

            row_numbers = [sp.alloc_register(f"first_row{n}") for n in range(2)]

            def first_rows(q):
                sp.load(row_numbers, slot_row[0:1, bass.ds(q * 2, 2)])
                return [sp.snap(number, min_val=0, max_val=E * REGION + (IDLE - 1) * P) for number in row_numbers]

            sp.wait_ge(S["late_wait_ready"], 1)
            late = [sp.value_load(late_wait[0:1, q:q + 1], min_val=1, max_val=2) for q in range(EARLY)]
            sp.wait_ge(S["dispatched"], 16 * (TILES - TPC) * TOPK)
            sp.wait_ge(S["table_row"], 1)

            def load(q, r, u):
                first_row = first_rows(q)
                if isinstance(q, int) and q < EARLY:
                    sp.wait_ge(S["late_rows"], late[q])
                elif isinstance(q, int) and q == EARLY:
                    sp.wait_ge(S["late_rows"], 2)
                after(sp, "yo_ready", q - BUFS + 1)
                for n in range(2):
                    sp.dma_start(xg[u][:, n, :], rows_d[bass.ds(first_row[n], P), :]).then_inc(S[f"xg_loaded{u}"], 16)

            rounds(sp, [(load, 0)], 1)
            sp.wait_ge(S["table_used"], 1)
            for k in range(TOPK):
                written = [nc.values_load(last_scatter[0:1, k, u:u + 1], engines=(mybir.EngineType.SP,), min_val=32,
                                          max_val=32 * PAIRS // BUFS) for u in range(BUFS)]
                for u in range(BUFS):
                    sp.wait_ge(S[f"scattered{u}"], written[u])
                res_v = res_d[k * TOKENS:(k + 1) * TOKENS, :].rearrange("(p t) d -> p t d", p=P)
                for c in range(CHUNKS):
                    sp.dma_start(o_all[:, k, tiles(c), :], res_v[:, tiles(c), :]).then_inc(S[f"o_in{k}_{c}"], 16)

        @block.gpsimd
        def _(pool):
            pool.memset(ident[:, :], 0.0).then_inc(S["zeroed"], 1)
            pool.memset(neg_half[:, :, :], -0.5).then_inc(S["halves"], 1)
            pool.memset(xn[:, :, 0:1], 0.0)
            pool.memset(yn[:, :, 0:1], 0.0).then_inc(S["late_rows"], 1)
            pool.memset(decay[:, :], 0.0).then_inc(S["zeroed"], 1)
            pool.wait_ge(S["zeroed"], 2)
            pool.affine_select(out=ident[:, :], in_=ident[:, :], compare_op=ALU.not_equal, fill=1.0, base=0,
                               pattern=[[-1, P]], channel_multiplier=1).then_inc(S["ident_ready"], 1)
            pool.memset(ones[:, :], 1.0).then_inc(S["consts"], 1)
            pool.memset(tri[:, :], 1.0).then_inc(S["consts"], 1)
            pool.memset(pad[:, :], 0.0).then_inc(S["pads"], 1)
            pool.wait_ge(S["pads"], 1)
            pool.memset(pad[:, D:D + 1].bitcast(I32), NOWHERE).then_inc(S["pads"], 1)
            pool.memset(ones_e[:, :], 1.0).then_inc(S["consts"], 1)
            pool.wait_ge(S["consts"], 2)
            pool.affine_select(out=tri[:, :], in_=tri[:, :], compare_op=ALU.is_gt, fill=0.0, base=0,
                               pattern=[[1, P]], channel_multiplier=-1).then_inc(S["consts"], 1)
            small = dict(channel_multiplier=0, allow_small_or_imprecise_dtypes=True)
            pool.iota(rev[:, :, :], pattern=[[0, TPC], [-1, E]], base=E, **small).then_inc(S["consts"], 1)
            pool.iota(region[:, :, :], pattern=[[0, TPC], [REGION, E]], base=0, **small).then_inc(S["consts"], 1)
            pool.iota(slot_no[:, :], pattern=[[1, SLOTS]], base=0, **small).then_inc(S["consts"], 1)
            pool.iota(pair_slot[:, :, :], pattern=[[2, BUFS], [2 * BUFS, PAIRS // BUFS]], base=0, **small)\
                .then_inc(S["consts"], 1)
            pool.iota(pair_end[:, :], pattern=[[2 * P, EARLY]], base=2 * P, **small).then_inc(S["consts"], 1)
            pool.iota(token_no[:, :], pattern=[[1, TILES]], base=0, channel_multiplier=TILES,
                      allow_small_or_imprecise_dtypes=True).then_inc(S["consts"], 1)
            pool.wait_ge(S["pads"], 2)
            pool.memset(pad[:, D + 1:D + 2], 0.0).then_inc(S["pads"], 1)
            pool.wait_ge(S["halves"], 1)

            def ln1_power(n):
                first, last = LN1_GROUPS[n]
                part = slice(first * TPC, last * TPC)
                pool.wait_ge(S["ln1_var"], last)
                pool.tensor_tensor(rs1[:, :, part], var1[:, :, part], neg_half[:, :, part], ALU.pow).then_inc(S["ln1_rstd"], 1)
                pool.wait_ge(S["ln1_rstd"], n + 1)
                pool.tensor_tensor(nm1[:, :, part], rs1[:, :, part],
                                   neg1[:, part].rearrange("p (o t) -> p o t", o=1).to_broadcast([P, 2, (last - first) * TPC]),
                                   ALU.mult).then_inc(S["nm1_ready"], 1)

            for n in range(len(LN1_GROUPS) - 1):
                ln1_power(n)

            def last_ln1_power(c):
                if isinstance(c, int) and c == 0:
                    ln1_power(len(LN1_GROUPS) - 1)

            def ln2_power(c):
                after(pool, "ln2_var", c + 1)
                after(pool, "z2_ready", c)
                pool.tensor_tensor(rs2[:, :], var2[:, :], neg_half[:, 0, 0:TPC], ALU.pow).then_inc(S["ln2_rstd"], 1)
                after(pool, "ln2_rstd", c + 1)
                pool.tensor_tensor(nm2[:, :], rs2[:, :], neg2[:, :], ALU.mult).then_inc(S["nm2_ready"], 1)

            def add_residual(c):
                after(pool, "x2_ready", c + 1)
                pool.tensor_tensor(x_all[:, tiles_of(c), :], x_all[:, tiles_of(c), :], x2[:, :, :], ALU.add)\
                    .then_inc(S["res_ready"], 1)

            def gate_sums(c):
                after(pool, "gate_r1", c + 1)
                after(pool, "num_ready", c + 1)
                after(pool, "rw_ready", c)
                pool.tensor_tensor(gated[:, :], tr[:, :], num[:, :], ALU.mult).then_inc(S["gated_ready"], 1)

            def add_ffn(c):
                after(pool, "ffn_ready", c + 1)
                after(pool, "res_ready", c + 1)
                after(pool, "x3_kept", 16 * c)
                after(pool, "xm_ready", c)
                pool.tensor_tensor(x3[:, :, :], ffn[:, :].rearrange("p (t d) -> p t d", t=TPC),
                                   x_all[:, tiles_of(c), :], ALU.add).then_inc(S["x3_ready"], 1)

            def shift_sum(c):
                after(pool, "yn_ready", c + 1)
                after(pool, "fk_done", FB * c)
                pool.tensor_tensor(ysum[:, :, :], yn[:, :, 1:L + 1], yn[:, :, 0:L], ALU.add)\
                    .then_inc(S["ysum_ready"], 1)

            def ln3_power(c):
                after(pool, "ln3_var", c + 1)
                after(pool, "xm_ready", c)
                pool.tensor_tensor(rs3[:, :], var3[:, :], neg_half[:, 0, 0:TPC], ALU.pow).then_inc(S["ln3_rstd"], 1)

            def dispatch(c, tiles):
                if 0 in tiles:
                    after(pool, "rows_copied", c + 1)
                    after(pool, "labelled", c + 1)
                    after(pool, "prob2", c + 1)
                    after(pool, "pos_ready", c + 1)
                for t in tiles:
                    for k in range(TOPK):
                        row = pos_of[is_last(c)][:, k, t:t + 1]
                        pool.indirect_dma_start(
                            out=rows_d[:, :], out_offset=bass.IndirectOffsetOnAxis(ap=row, axis=0),
                            in_=rows_of[is_last(c)][:, t, k, :], in_offset=None, bounds_check=c + E * REGION, oob_is_err=False)\
                            .then_inc(S["last_dispatched" if is_last(c) else "dispatched"], 16)

            def dispatch_first(c):
                dispatch(c, [0, 1])

            def dispatch_second(c):
                dispatch(c, [2, 3])

            pipeline(pool, [(add_ffn, 3), (shift_sum, 2), (add_residual, 2), (ln3_power, 3), (last_ln1_power, 2),
                            (dispatch_first, 4), (ln2_power, 1), (dispatch_second, 4), (gate_sums, 0)])

            pool.wait_ge(S["last_dispatched"], 16 * TPC * TOPK)
            pool.wait_ge(S["pad_filled"], 16 * E)
            pool.wait_ge(S["idle_filled"], 16)
            pool.memset(late_mark[:, :], 0.0).then_inc(S["late_rows"], 1)

            def scatter(q, r, u):
                after(pool, "yo_ready", q + 1)
                for n in range(2):
                    row = result_row[u][:, n:n + 1]
                    pool.indirect_dma_start(
                        out=res_d[:, :], out_offset=bass.IndirectOffsetOnAxis(ap=row, axis=0),
                        in_=yo[u][:, n, :], in_offset=None, bounds_check=q + RESULTS, oob_is_err=False)\
                        .then_inc(S[f"scattered{u}"], 16)

            rounds(pool, [(scatter, 0)], 0)
            pool.wait_ge(S["x3_kept"], 16 * CHUNKS)
            for c in range(DVE_CHUNKS, CHUNKS):
                add_result(pool, 0, c, "lower_added_pool")
            for u in range(BUFS):
                pool.wait_ge(S[f"scattered{u}"], 32 * PAIRS // BUFS)

        @block.scalar
        def _(act):
            act.dma_start(vec[:, :], v_in).then_inc(S["vecs_in"], 16)
            act.dma_start(w_sb[:, :], w_in).then_inc(S["weights_in"], 16)
            act.dma_start(w_exp[:, :], experts_in).then_inc(S["experts_in"], 16)
            act.wait_ge(S["pads"], 3)
            act.dma_start(rows_d[E * REGION:, :].rearrange("(k p) w -> p k w", p=P),
                          pad[:, :].rearrange("p (o w) -> p o w", o=1).to_broadcast([P, IDLE, ROW])).then_inc(S["idle_filled"], 16)
            act.wait_ge(S["vecs_in"], 16)
            act.activation(ew[:, 0:1], V("time_decay"), ACT.Exp).then_inc(S["ew_ready"], 1)
            act.wait_ge(S["ew_ready"], 1)
            act.activation(ew[:, 1:2], ew[:, 0:1], ACT.Exp, scale=-1.0).then_inc(S["ew2_ready"], 1)
            act.wait_ge(S["zeroed"], 2)
            act.wait_ge(S["ew2_ready"], 1)
            dv = decay[:, :].rearrange("p (b l) -> p b l", b=BPC)
            act.activation(dv[:, :, 1:L], dv[:, :, 1:L], ACT.Identity, bias=ew[:, 1:2]).then_inc(S["decay_ready"], 1)
            mix = vec[:, VEC["mix_k"]:VEC["mix_k"] + 3]
            act.activation(rest_mix[:, :], mix, ACT.Copy, scale=-1.0, bias=1.0).then_inc(S["mix_rest_ready"], 1)
            act.wait_ge(S["mix_rest_ready"], 1)
            act.wait_ge(S["weights_in"], 16)
            for n, w in enumerate(["Wk", "Wv", "Wr"]):
                act.activation(w_mix[:, n, 0, :], W(w), ACT.Copy, scale=mix[:, n:n + 1])
                act.activation(w_mix[:, n, 1, :], W(w), ACT.Copy, scale=rest_mix[:, n:n + 1]).then_inc(S["w_mixed"], 1)
            act.activation(wfv_half[:, :], W("Wfv"), ACT.Copy, scale=0.5).then_inc(S["w_mixed"], 1)

            def normed_x(c):
                after(act, "z1_T", c + 1)
                after(act, "r_done", c)
                act.activation(xn[:, :, 1:L + 1], p_tr[:, :].rearrange("p (b l) -> p b l", b=BPC), ACT.Identity,
                               bias=V("ln1_b"), scale=V("ln1_g")).then_inc(S["xn_ready"], 1)

            def first_apply(c):
                after_ln1(act, c)
                after(act, "z1_T", c)
                after(act, "z1_wait_taken", c)
                act.activation(z1_wait[:, :], V("mix_k"), ACT.Copy).then_inc(S["z1_wait_taken"], 1)
                for t in range(TPC):
                    xt = x_all[:, bass.ds(c * TPC + t, 1), :].rearrange("p o d -> p (o d)")
                    last = act.activation(z1[:, t, :], xt, ACT.Identity, scale=rs1[:, 1, bass.ds(c * TPC + t, 1)],
                                          bias=nm1[:, 1, bass.ds(c * TPC + t, 1)])
                last.then_inc(S["z1_ready"], 1)

            def first_norm(c):
                after_ln1(act, c)
                after(act, "x2_ready", c)
                after(act, "y1_wait_taken", c)
                act.activation(y1_wait[:, :], V("mix_k"), ACT.Copy).then_inc(S["y1_wait_taken"], 1)
                for t in range(TPC):
                    xt = x_all[:, bass.ds(c * TPC + t, 1), :].rearrange("p o d -> p (o d)")
                    last = act.activation(y1[:, t, :], xt, ACT.Identity, scale=rs1[:, 0, bass.ds(c * TPC + t, 1)],
                                          bias=nm1[:, 0, bass.ds(c * TPC + t, 1)])
                last.then_inc(S["y1_ready"], 1)

            def second_apply(c):
                after(act, "nm2_ready", c + 1)
                after(act, "z2_T", c)
                for t in range(TPC):
                    last = act.activation(z2[:, t, :], x2[:, t, :], ACT.Identity, scale=rs2[:, t:t + 1],
                                          bias=nm2[:, t:t + 1])
                last.then_inc(S["z2_ready"], 1)

            def exps(c):
                after(act, "k_done", c + 1)
                after(act, "den_ready", c)
                pk = p_k[:, :].rearrange("p (b l) -> p b l", b=BPC)
                act.activation(ek[:, :, 0:1], pk[:, :, 0:1], ACT.Exp, bias=V("time_first"))
                act.activation(ek[:, :, 1:L], pk[:, :, 1:L], ACT.Exp).then_inc(S["exp_done"], 1)

            def tanh_r(c):
                after(act, "r_done", c + 1)
                after(act, "gated_ready", c)
                act.activation(tr[:, :], p_r[:, :], ACT.Tanh, scale=0.5).then_inc(S["gate_r"], 1)
                after(act, "gate_r", c + 1)
                act.activation(tr[:, :], tr[:, :], ACT.Copy, bias=1.0).then_inc(S["gate_r1"], 1)

            def normed_y(c):
                after(act, "z2_T", c + 1)
                after(act, "ysum_ready", c)
                after(act, "rr_done", c)
                act.activation(yn[:, :, 1:L + 1], p_tr[:, :].rearrange("p (b l) -> p b l", b=BPC), ACT.Identity,
                               bias=V("ln2_b"), scale=V("ln2_g")).then_inc(S["yn_ready"], 1)

            def gate_y(c):
                after(act, "rr_done", c + 1)
                after(act, "ffn_ready", c)
                act.activation(trr[:, :], p_tok[:, :], ACT.Tanh, scale=0.5).then_inc(S["trr_ready"], 1)

            def relu(f):
                def step(c):
                    after(act, "fv_done", FB * (c - 1) + f + 1)
                    after(act, "fk_done", FB * c + f + 1)
                    act.activation(hr[:, f, :], p_h[f % 2][:, :], ACT.Relu, scale=0.5).then_inc(S["relu_done"], 1)
                return step

            def square(f):
                def step(c):
                    after(act, "relu_done", FB * c + f + 1)
                    act.activation(kk[:, f, :], hr[:, f, :], ACT.Square).then_inc(S["kk_ready"], 1)
                return step

            def normed_m(c):
                after(act, "xm_T", c + 1)
                after(act, "scores_done", c)
                act.activation(xmT[:, :], p_tr[:, :], ACT.Copy).then_inc(S["xmT_ready"], 1)

            def copy_rows(c):
                after(act, "xm_ready", c + 1)
                after_dispatched(act, c)
                twice = xm[:, :, :].rearrange("p t (o d) -> p t o d", o=1).to_broadcast([P, TPC, TOPK, D])
                act.activation(rows_of[is_last(c)][:, :, :, 0:D], twice, ACT.Copy).then_inc(S["rows_copied"], 1)

            def gap_exp(c):
                after(act, "gap_ready", c + 1)
                after(act, "prob2", c)
                act.activation(egap[:, :], gap[:, :], ACT.Exp).then_inc(S["egap_ready"], 1)

            pipeline(act, [(relu(0), 4), (square(0), 4), (tanh_r, 2), (normed_m, 5), (relu(1), 4), (square(1), 4),
                           (relu(2), 4), (square(2), 4), (normed_x, 1), (relu(3), 4), (square(3), 4),
                           (second_apply, 3), (gap_exp, 5), (exps, 1), (normed_y, 3), (copy_rows, 5),
                           (first_apply, 0), (gate_y, 3), (first_norm, 2)])

            act.wait_ge(S["total_int"], 1)
            fill_pads(act, range(1, E, 2))

            loaded = [act.alloc_register(f"first_col{n}") for n in range(2)]
            act.wait_ge(S["table_w"], 1)
            act.wait_ge(S["experts_in"], 16)

            def tanh(q, _, u):
                after(act, "up_done", q + 1)
                after(act, "gate_h_ready", q)
                act.activation(th[:, :, :], p_up[u % 2][:, :, 0:H], ACT.Tanh, scale=0.5).then_inc(S["tanh_ready"], 1)

            def turned_rows(q, _, u):
                after(act, "xg_T", q + 1)
                after(act, "up_done", q - 1)
                act.activation(xgT[u % 2][:, :, :], p_tr[:, 0:2 * P].rearrange("p (n m) -> p n m", n=2), ACT.Copy)\
                    .then_inc(S["xgT_ready"], 1)

            def expert_weights(q, _, u):
                act.load(loaded, slot_w[0:1, bass.ds(q * 2, 2)])
                for n in range(2):
                    first_col = act.snap(loaded[n], min_val=0, max_val=(E - 1) * EW)
                    act.activation(w_up[u % 2][:, n, :], w_exp[:, bass.ds(first_col, 2 * H)], ACT.Copy)

            def next_expert_weights(q, r, u):
                if not isinstance(q, int) or q >= 2:
                    expert_weights(q, r, u)

            for q in range(2):
                expert_weights(q, 0, q)
            rounds(act, [(turned_rows, -1), (tanh, 0), (next_expert_weights, -2)], 1)
            for c in range(CHUNKS):
                act.wait_ge(S["higher_added"], c + 1)
                act.dma_start(out[:, tiles(c), :], x_all[:, tiles(c), :]).then_inc(S["stored"], 16)
            act.wait_ge(S["stored"], 16 * CHUNKS)

        @block.tensor
        def _(pe):
            pe.wait_ge(S["ident_ready"], 1)
            pe.wait_ge(S["weights_in"], 16)
            pe.wait_ge(S["consts"], 10)

            def warm_up(products, unread):
                for _ in range(products):
                    pe.matmul(unread[:, :], ident[:, :], W("Wfk"), start=True, stop=True)

            warm_up(1, p_f)
            pe.wait_ge(S["w_mixed"], 4)

            def turn_tiles(src, done):
                for t in range(TPC):
                    mm = pe.transpose(p_tr[:, t * P:(t + 1) * P], src[:, t, :], ident[:, :])
                mm.then_inc(S[done], 1)

            def turn_x(c):
                after(pe, "z1_ready", c + 1)
                after(pe, "xmT_ready", c - 3)
                if isinstance(c, int):
                    after(pe, "yn_ready", c - 2)
                    after(pe, "xn_ready", c)
                turn_tiles(z1, "z1_T")

            def project(n, p_out, done, guards):
                def step(c):
                    after(pe, "xn_ready", c + 1)
                    for name, count in guards(c):
                        after(pe, name, count)
                    o = p_out[:, :].rearrange("p (b l) -> p b l", b=BPC)
                    pe.matmul(o, w_mix[:, n, 0, :], xn[:, :, 1:L + 1], start=True, stop=False)
                    pe.matmul(o, w_mix[:, n, 1, :], xn[:, :, 0:L], start=False, stop=True).then_inc(S[done], 1)
                return step

            k_in = project(0, p_k, "k_done", lambda c: [("exp_done", c)])
            v_in = project(1, p_v, "v_done", lambda c: [("ekv_ready", c)])
            r_in = project(2, p_r, "r_done", lambda c: [("gate_r", c), ("spot_ready", c - 3)])

            def attn_out(c):
                after(pe, "rw_ready", c + 1)
                after(pe, "trr_ready", c)
                for t in range(TPC):
                    mm = pe.matmul(p_tok[:, t * P:(t + 1) * P], rw[:, t * P:(t + 1) * P], W("Wo"),
                                   start=True, stop=True)
                mm.then_inc(S["wo_done"], 1)

            def turn_y(c):
                after(pe, "z2_ready", c + 1)
                after(pe, "xn_ready", upto(c + 3))
                if isinstance(c, int):
                    after(pe, "xmT_ready", c - 1)
                turn_tiles(z2, "z2_T")

            def gate_in(c):
                after(pe, "yn_ready", c + 1)
                after(pe, "x2_ready", c + 1)
                for t in range(TPC):
                    tile = yn[:, t // 2, 1 + (t % 2) * P:1 + (t % 2 + 1) * P]
                    mm = pe.matmul(p_tok[:, t * P:(t + 1) * P], tile, W("Wfr"), start=True, stop=True)
                mm.then_inc(S["rr_done"], 1)

            def ffn_in(f):
                def step(c):
                    after(pe, "ysum_ready", c + 1)
                    after(pe, "relu_done", FB * c + f - 1)
                    pe.matmul(p_h[f % 2][:, :], W("Wfk")[:, f * P:(f + 1) * P],
                              ysum[:, :, :].rearrange("p b l -> p (b l)"), start=True, stop=True)\
                        .then_inc(S["fk_done"], 1)
                return step

            def ffn_out(f):
                def step(c):
                    after(pe, "kk_ready", FB * c + f + 1)
                    if f == 0:
                        after(pe, "ffn_ready", c)
                    for t in range(TPC):
                        mm = pe.matmul(p_f[:, t * P:(t + 1) * P], kk[:, f, t * P:(t + 1) * P],
                                       wfv_half[:, f * P:(f + 1) * P],
                                       start=(f == 0 and t == 0), stop=(f == FB - 1 and t == TPC - 1))
                    mm.then_inc(S["fv_done"], 1)
                return step

            def turn_m(c):
                if is_last(c):
                    after(pe, "trr_ready", CHUNKS)
                    warm_up(3, p_tok)
                after(pe, "xm_ready", c + 1)
                after(pe, "yn_ready", upto(c + 2))
                if isinstance(c, int):
                    after(pe, "xmT_ready", c)
                turn_tiles(xm, "xm_T")

            def scores(c):
                after(pe, "xmT_ready", c + 1)
                after(pe, "gate_r", upto(c + 4))
                if isinstance(c, int):
                    after(pe, "spot_ready", c)
                for t in range(TPC):
                    mm = pe.matmul(p_r[:, t * E:(t + 1) * E], xmT[:, t * P:(t + 1) * P], W("gate"), start=True, stop=True)
                mm.then_inc(S["scores_done"], 1)

            def ranks(c):
                after(pe, "both_ready", c + 1)
                after(pe, "scores_in", c + 1)
                r = p_r[:, 0:TPC * E].rearrange("p (t e) -> p t e", t=TPC)
                after(pe, "seen_ready", c + 1)
                pe.matmul(r, tri[:, :], both[:, :, :], start=True, stop=False)
                for t in range(TPC - 1):
                    pe.matmul(r[:, t + 1:, :], ones[:, :], both[:, t:t + 1, :].to_broadcast([P, TPC - 1 - t, E]),
                              start=False, stop=False)
                pe.matmul(r, ones[:, :], seen[:, :].rearrange("p (o e) -> p o e", o=1).to_broadcast([P, TPC, E]),
                          start=False, stop=True).then_inc(S["rank_done"], 1)

            pipeline(pe, [(gate_in, 3), (r_in, 1), (ffn_in(0), 3), (attn_out, 2), (ffn_in(1), 3), (ffn_in(2), 3),
                          (turn_m, 4), (ffn_out(0), 3), (turn_x, 0), (scores, 4), (ffn_in(3), 3), (ffn_out(1), 3),
                          (ffn_out(2), 3), (ffn_out(3), 3), (k_in, 0), (turn_y, 2), (ranks, 4), (v_in, 0)])

            pe.wait_ge(S["seen_ready"], CHUNKS + 1)
            pe.wait_ge(S["spot_ready"], CHUNKS)
            pe.matmul(p_r[:, 0:E], ones[:, :], seen[:, :], start=True, stop=True).then_inc(S["total_done"], 1)

            pe.wait_ge(S["table_w"], 1)
            warm_up(4, p_f)
            pe.wait_ge(S["experts_in"], 16)
            loaded = [pe.alloc_register(f"first_col{n}") for n in range(2)]

            def turn_rows(q, r, u):
                after(pe, f"xg_loaded{u}", r * 32 + 32)
                after(pe, "xgT_ready", q)
                for n in range(2):
                    mm = pe.transpose(p_tr[:, n * P:(n + 1) * P], xg[u][:, n, 0:D], ident[:, :])
                mm.then_inc(S["xg_T"], 1)

            def up(q, _, u):
                after(pe, "xgT_ready", q + 1)
                for n in range(2):
                    for h in range(2 * H // P):
                        mm = pe.matmul(p_up[u % 2][:, n, h * P:(h + 1) * P], w_up[u % 2][:, n, h * P:(h + 1) * P],
                                       xgT[u % 2][:, n, :], start=True, stop=True)
                mm.then_inc(S["up_done"], 1)

            def down(q, _, u):
                pe.load(loaded, slot_w[0:1, bass.ds(q * 2, 2)])
                first_col = [pe.snap(value, min_val=0, max_val=(E - 1) * EW) for value in loaded]
                after(pe, "hid_ready", q + 1)
                after(pe, "yo_ready", q - 1)
                for n in range(2):
                    for j in range(2):
                        mm = pe.matmul((p_r, p_f)[u % 2][:, n * D:(n + 1) * D], hid[u % 2][:, n, j, :],
                                       w_exp[:, bass.ds(first_col[n] + (2 * H + j * D), D)],
                                       start=(j == 0), stop=(j == 1))
                mm.then_inc(S["down_done"], 1)

            rounds(pe, [(turn_rows, -1), (up, 0), (down, 1)], 1)

        @block.vector
        def _(dve):
            dve.memset(seen[:, :], 0.0).then_inc(S["seen_ready"], 1)

            def moments(src, st, mv, which, c):
                for t in range(TPC):
                    last = dve.bn_stats(st[:, t, :], src(t))
                last.then_inc(S[which + "_stats"], 1)
                after(dve, which + "_stats", c + 1)
                w = int(which[2]) - 1
                dve.tensor_copy(moments_wait[:, w:w + 1], st[:, TPC - 1, 0:1])
                for t in range(TPC):
                    last = dve.bn_aggr(mv[:, t, :], st[:, t, :])
                last.then_inc(S[which + "_moments"], 1)
                after(dve, which + "_moments", c + 1)

            def ln1(c):
                if isinstance(c, int) and c < 2:
                    dve.wait_ge(S["x_first" if c == 0 else "x_second"], 16)
                else:
                    dve.wait_ge(S["x_rest"], 16)
                moments(lambda t: x_all[:, bass.ds(c * TPC + t, 1), :].rearrange("p o d -> p (o d)"), st1, mv1, "ln1", c)
                dve.tensor_scalar(neg1[:, tiles_of(c)], mv1[:, :, 0], -1.0, None, ALU.mult)
                dve.tensor_scalar(var1[:, 0, tiles_of(c)], mv1[:, :, 1], LN_EPS, None, ALU.add)
                dve.tensor_scalar(var1[:, 1, tiles_of(c)], mv1[:, :, 1], 1.0 + LN_EPS, LN_EPS * LN_EPS, ALU.mult, ALU.add)\
                    .then_inc(S["ln1_var"], 1)

            def ln1_group(n):
                first, last = LN1_GROUPS[n]
                if last - first == 1:
                    ln1(first)
                else:
                    with dve.Fori(first, last) as c:
                        ln1(c)

            for n in range(len(LN1_GROUPS) - 1):
                ln1_group(n)

            def last_ln1(c):
                if isinstance(c, int) and c == 0:
                    ln1_group(len(LN1_GROUPS) - 1)

            dve.wait_ge(S["decay_ready"], 1)
            dve.wait_ge(S["consts"], 10)

            def wkv_sums(c):
                after(dve, "exp_done", c + 1)
                after(dve, "v_done", c + 1)
                ekf = ek[:, :, :].rearrange("p b l -> p (b l)")
                dve.tensor_tensor(ekv[:, :], ekf, p_v[:, :], ALU.mult).then_inc(S["ekv_ready"], 1)
                dve.tensor_tensor_scan(den[:, :], decay[:, :], ekf, 0.0, ALU.mult, ALU.add).then_inc(S["den_ready"], 1)
                after(dve, "den_ready", c + 1)
                dve.tensor_scalar(den[:, :], den[:, :], WKV_EPS, None, ALU.add).then_inc(S["den_eps"], 1)
                after(dve, "ekv_ready", c + 1)
                dve.tensor_tensor_scan(num[:, :], decay[:, :], ekv[:, :], 0.0, ALU.mult, ALU.add)\
                    .then_inc(S["num_ready"], 1)

            def invert(c):
                after(dve, "den_eps", c + 1)
                dve.reciprocal(rden[:, :], den[:, :]).then_inc(S["rden_ready"], 1)

            def receptance(c):
                after(dve, "gated_ready", c + 1)
                after(dve, "rden_ready", c + 1)
                after(dve, "wo_done", c)
                dve.tensor_tensor(rw[:, :], gated[:, :], rden[:, :], ALU.mult).then_inc(S["rw_ready"], 1)

            def ln2(c):
                after(dve, "wo_done", c + 1)
                after(dve, "y1_ready", c + 1)
                after(dve, "res_ready", c)
                dve.scalar_tensor_tensor(out=x2[:, :, :], in0=p_tok[:, :].rearrange("p (t d) -> p t d", t=TPC),
                                         scalar=0.5, in1=y1[:, :, :], op0=ALU.mult, op1=ALU.add)\
                    .then_inc(S["x2_ready"], 1)
                after(dve, "x2_ready", c + 1)
                moments(lambda t: x2[:, t, :], st2, mv2, "ln2", c)
                after(dve, "nm2_ready", c)
                dve.tensor_scalar(neg2[:, :], mv2[:, :, 0], -1.0, None, ALU.mult)
                dve.tensor_scalar(var2[:, :], mv2[:, :, 1], LN_EPS, None, ALU.add).then_inc(S["ln2_var"], 1)

            def gated_ffn(c):
                after(dve, "fv_done", FB * (c + 1))
                after(dve, "trr_ready", c + 1)
                after(dve, "x3_ready", c)
                dve.scalar_tensor_tensor(out=ffn[:, :], in0=trr[:, :], scalar=1.0, in1=p_f[:, :],
                                         op0=ALU.add, op1=ALU.mult).then_inc(S["ffn_ready"], 1)

            def ln3(c):
                after(dve, "x3_ready", c + 1)
                moments(lambda t: x3[:, t, :], st3, mv3, "ln3", c)
                after(dve, "ln3_rstd", c)
                dve.tensor_scalar(var3[:, :], mv3[:, :, 1], LN_EPS, None, ALU.add).then_inc(S["ln3_var"], 1)

            def ln3_apply(c):
                after(dve, "ln3_rstd", c + 1)
                after(dve, "xm_T", c)
                after(dve, "rows_copied", c)
                for t in range(TPC):
                    last = dve.tensor_scalar(xm[:, t, :], x3[:, t, :], mv3[:, t, 0:1], rs3[:, t:t + 1],
                                             ALU.subtract, ALU.mult)
                last.then_inc(S["xm_ready"], 1)

            def flat(ap, o):
                return ap.rearrange("p (t o) -> p t o", o=1).to_broadcast([P, TPC, E])

            PICKS = 10

            def picked(c, ins, n):
                ins.then_inc(S["picking"], 1)
                after(dve, "picking", c * PICKS + n)

            def pick_one(c, k, n, sc):
                picked(c, dve.tensor_reduce(best[:, k, :], sc, mybir.AxisListType.X, ALU.max), n + 1)
                picked(c, dve.tensor_tensor(eq[:, :, :], sc, flat(best[:, k, :], E), ALU.is_equal), n + 2)
                picked(c, dve.tensor_tensor(eq[:, :, :], eq[:, :, :], rev[:, :, :], ALU.mult), n + 3)
                picked(c, dve.tensor_reduce(low[:, k, :], eq[:, :, :], mybir.AxisListType.X, ALU.max), n + 4)
                picked(c, dve.tensor_tensor(hot[:, k, :, :], rev[:, :, :], flat(low[:, k, :], E), ALU.is_equal), n + 5)

            def pick(c):
                after(dve, "scores_done", c + 1)
                scores = p_r[:, 0:TPC * E].rearrange("p (t e) -> p t e", t=TPC)
                pick_one(c, 0, 0, scores)
                dve.scalar_tensor_tensor(out=sc[:, :, :], in0=hot[:, 0, :, :], scalar=-3.0e38, in1=scores,
                                         op0=ALU.mult, op1=ALU.add).then_inc(S["scores_in"], 1)
                after(dve, "scores_in", c + 1)
                pick_one(c, 1, 5, sc[:, :, :])
                after(dve, "rank_done", c)
                dve.tensor_tensor(both[:, :, :], hot[:, 0, :, :], hot[:, 1, :, :], ALU.add).then_inc(S["both_ready"], 1)
                dve.tensor_tensor(gap[:, :], best[:, 1, :], best[:, 0, :], ALU.subtract).then_inc(S["gap_ready"], 1)

            def place(c):
                after(dve, "rank_done", c + 1)
                dve.tensor_tensor(spot[:, :, :], region[:, :, :], p_r[:, 0:TPC * E].rearrange("p (t e) -> p t e", t=TPC),
                                  ALU.add).then_inc(S["spot_ready"], 1)
                with nc.allow_low_precision(reason="whole numbers up to TPC"):
                    dve.tensor_reduce(chunk_seen[:, :], both[:, :, :].rearrange("p t e -> p e t"), mybir.AxisListType.X,
                                      ALU.add).then_inc(S["chunk_seen_ready"], 1)
                after(dve, "spot_ready", c + 1)
                for k in range(TOPK):
                    last = dve.tensor_tensor(spots[:, k, :, :], hot[:, k, :, :], spot[:, :, :], ALU.mult)
                last.then_inc(S["spots_ready"], 1)
                after(dve, "chunk_seen_ready", c + 1)
                dve.tensor_tensor(seen[:, :], seen[:, :], chunk_seen[:, :], ALU.add).then_inc(S["seen_ready"], 1)
                after(dve, "spots_ready", c + 1)
                after_dispatched(dve, c)
                with nc.allow_low_precision(reason="whole numbers under 2**24, summed in float32"):
                    dve.tensor_reduce(pos_of[is_last(c)][:, :, :], spots[:, :, :, :], mybir.AxisListType.X, ALU.add)\
                        .then_inc(S["pos_ready"], 1)

            def label(c):
                after(dve, "egap_ready", c + 1)
                dve.tensor_scalar(esum[:, :], egap[:, :], 1.0, None, ALU.add).then_inc(S["esum_ready"], 1)
                dve.tensor_tensor(higher[:, 0, :], low[:, 0, :], low[:, 1, :], ALU.is_lt)
                dve.tensor_tensor(higher[:, 1, :], low[:, 1, :], low[:, 0, :], ALU.is_lt).then_inc(S["order_known"], 1)
                after(dve, "order_known", c + 1)
                after_dispatched(dve, c)
                rows = rows_of[is_last(c)]
                for k in range(TOPK):
                    last = dve.scalar_tensor_tensor(out=rows[:, :, k, D].bitcast(I32), in0=higher[:, k, :],
                                                    scalar=float(TOKENS), in1=token_no[:, tiles_of(c)],
                                                    op0=ALU.mult, op1=ALU.add)
                last.then_inc(S["labelled"], 1)
                after(dve, "esum_ready", c + 1)
                dve.reciprocal(prob[:, :, 0], esum[:, :]).then_inc(S["prob1"], 1)
                after(dve, "prob1", c + 1)
                dve.tensor_copy(rows[:, :, 0, D + 1], prob[:, :, 0])
                dve.tensor_tensor(rows[:, :, 1, D + 1], prob[:, :, 0], egap[:, :], ALU.mult).then_inc(S["prob2"], 1)

            pipeline(dve, [(place, 4), (ln3, 3), (last_ln1, 2), (label, 4), (wkv_sums, 0), (ln3_apply, 3), (ln2, 1),
                           (invert, 0), (pick, 3), (gated_ffn, 2), (receptance, 0)])

            steps_made = [0]

            def link(ins):
                steps_made[0] += 1
                ins.then_inc(S["table_steps"], 1)
                dve.wait_ge(S["table_steps"], steps_made[0])

            dve.wait_ge(S["total_done"], 1)
            link(dve.tensor_copy(total[:, :], p_r[:, 0:E]))
            dve.tensor_copy(total_i[:, :], total[:, :]).then_inc(S["total_int"], 1)
            link(dve.tensor_scalar(is_late[:, :], pair_end[:, :], spot[:, 0, 0:1], None, ALU.is_gt))
            dve.tensor_scalar(late_wait[:, :], is_late[:, :], 1.0, None, ALU.add)\
                .then_inc(S["late_wait_ready"], 1)
            link(dve.tensor_scalar(ntile_i[:, :], total[:, :], float(P - 1), None, ALU.add))
            link(dve.tensor_scalar(ntile_i[:, :], ntile_i[:, :], P.bit_length() - 1, None, ALU.arith_shift_right))
            link(dve.tensor_copy(ntile[:, :], ntile_i[:, :]))
            link(dve.tensor_tensor_scan(cum[:, :], ones_e[:, :], ntile[:, :], 0.0, ALU.mult, ALU.add))
            over_e = lambda ap: ap.rearrange("p (s o) -> p s o", o=1).to_broadcast([P, SLOTS, E])
            over_s = lambda ap: ap.rearrange("p (o e) -> p o e", o=1).to_broadcast([P, SLOTS, E])
            link(dve.tensor_tensor(past[:, :, :], over_e(slot_no[:, :]), over_s(cum[:, :]), ALU.is_ge))
            link(dve.tensor_reduce(slot_e[:, :], past[:, :, :], mybir.AxisListType.X, ALU.add))
            dve.tensor_scalar(slot_w[:, :], slot_e[:, :], float(E - 1), float(EW), ALU.min, ALU.mult)\
                .then_inc(S["table_w"], 1)
            link(dve.tensor_tensor(past_tiles[:, :, :], past[:, :, :], over_s(ntile[:, :]), ALU.mult))
            link(dve.tensor_reduce(slot_first[:, :], past_tiles[:, :, :], mybir.AxisListType.X, ALU.add))
            link(dve.tensor_tensor(slot_first[:, :], slot_no[:, :], slot_first[:, :], ALU.subtract))
            link(dve.tensor_scalar(slot_first[:, :], slot_first[:, :], float(P), None, ALU.mult))
            dve.scalar_tensor_tensor(out=slot_row[:, :], in0=slot_e[:, :], scalar=float(REGION), in1=slot_first[:, :],
                                     op0=ALU.mult, op1=ALU.add).then_inc(S["table_row"], 1)
            for k in range(TOPK):
                tiles_until = cum[:, E - TOPK + k:E - TOPK + k + 1]
                last = dve.tensor_scalar(used[:, k, :, :], pair_slot[:, :, :], tiles_until, None, ALU.is_lt)
            link(last)
            link(dve.tensor_reduce(rounds_used[:, :, :], used[:, :, :, :], mybir.AxisListType.X, ALU.add))
            dve.tensor_scalar(last_scatter[:, :, :], rounds_used[:, :, :], 1.0, 32.0, ALU.max, ALU.mult)\
                .then_inc(S["table_used"], 1)

            def gate_hidden(q, _, u):
                after(dve, "tanh_ready", q + 1)
                after(dve, "hid_ready", q)
                dve.scalar_tensor_tensor(out=gate_h[:, :, :], in0=th[:, :, :], scalar=1.0, in1=p_up[u % 2][:, :, 0:H],
                                         op0=ALU.add, op1=ALU.mult).then_inc(S["gate_h_ready"], 1)
                after(dve, "gate_h_ready", q + 1)
                after(dve, "down_done", q - 1)
                dve.tensor_tensor(hid[u % 2][:, :, :, :].rearrange("p n j m -> p n (j m)"), gate_h[:, :, :],
                                  p_up[u % 2][:, :, H:2 * H], ALU.mult).then_inc(S["hid_ready"], 1)

            def weigh(q, r, u):
                after(dve, "down_done", q + 1)
                after(dve, f"scattered{u}", r * 32)
                dve.tensor_copy(result_row[u][:, :].rearrange("p (n o) -> p n o", o=1),
                                xg[u][:, :, D:D + 1].bitcast(U32))
                for n in range(2):
                    last = dve.tensor_scalar(yo[u][:, n, :], (p_r, p_f)[u % 2][:, n * D:(n + 1) * D],
                                             xg[u][:, n, D + 1:D + 2], 0.5, ALU.mult, ALU.mult)
                last.then_inc(S["yo_ready"], 1)

            rounds(dve, [(gate_hidden, 0), (weigh, 1)], 2)

            dve.wait_ge(S["x3_kept"], 16 * CHUNKS)
            for c in range(DVE_CHUNKS):
                add_result(dve, 0, c, "lower_added")
            for c in range(CHUNKS):
                if c < DVE_CHUNKS:
                    dve.wait_ge(S["lower_added"], c + 1)
                else:
                    dve.wait_ge(S["lower_added_pool"], c - DVE_CHUNKS + 1)
                add_result(dve, 1, c, "higher_added")


def kernel(**inputs):
    import numpy as np
    import concourse.bacc as bacc
    from concourse.bass_utils import run_bass_kernel_spmd as run

    a = {k.replace("L0_attn_", "").replace("L0_ffn_", ""): np.asarray(v) for k, v in inputs.items()}
    arrays = {
        "x": a["x"].reshape(TILES, P, D).transpose(1, 0, 2),
        "weights": np.concatenate([a["Wk"], a["Wv"], a["Wr"], a["Wo"], a["Wfr"], a["Wfk"],
                                   a["Wfv"].reshape(FB, P, D).transpose(1, 0, 2).reshape(P, FFN),
                                   a["gate_w"].T], axis=1),
        "vecs": np.stack([a[n] for n in VEC], axis=1),
        "experts": np.concatenate([a["w12"].transpose(2, 0, 1),
                                   a["w3"].transpose(2, 0, 1).reshape(2, P, E, D).transpose(1, 2, 0, 3).reshape(P, E, 2 * D)],
                                  axis=2).reshape(P, E * EW),
    }
    arrays = {k: np.ascontiguousarray(v) for k, v in arrays.items()}
    nc = bacc.Bacc("TRN2", target_bir_lowering=False, num_devices=1)
    args = [nc.dram_tensor(k, v.shape, F32, kind="ExternalInput").ap() for k, v in arrays.items()]
    args.append(nc.dram_tensor("out", [P, TILES, D], F32, kind="ExternalOutput").ap())
    build(nc, *args)
    r = run(nc, [arrays], core_ids=[0])
    return r.results[0]["out"].transpose(1, 0, 2).reshape(B, L, D)
```
